# Optimizing a Trainium2 kernel written in Bass

```python
import numpy as np
import jax
import jax.numpy as jnp

def _softmax(x, axis=-1):
    return jax.nn.softmax(x, axis=axis)

def _gelu(x):
    return jax.nn.gelu(x, approximate=True)

def _silu(x):
    return jax.nn.silu(x)

def _sigmoid(x):
    return jax.nn.sigmoid(x)

def _layernorm(x, axis=-1, eps=1e-05):
    m = jnp.mean(x, axis=axis, keepdims=True)
    v = jnp.var(x, axis=axis, keepdims=True)
    return (x - m) / jnp.sqrt(v + eps)

def _scatter_add(tgt, idx, src, axis=0):
    return tgt.at[idx].add(src)

def _segment_sum(src, seg, n):
    return jax.ops.segment_sum(src, seg, n)
kernel_name = 'mk_seq_postln_d1_jaxref_r4_45abce'

def setup_inputs(seed: int=0):
    np.random.seed(seed)
    _w = jnp.asarray

    def _L0_attn_setup():
        import jax, jax.numpy as jnp
        import numpy as np
        D_MODEL = 256
        N_HEADS = 16
        D_K = 64
        SEQ = 1024
        BATCH = 1

        def _rope(x):
            d = x.shape[-1]
            d2 = d // 2
            theta = 1.0 / 10000.0 ** (jnp.arange(0, d, 2, dtype=jnp.float32) / d)
            pos = jnp.arange(x.shape[1], dtype=jnp.float32)
            idx_theta = pos[:, None] * theta[None, :]
            idx_theta2 = jnp.concatenate([idx_theta, idx_theta], axis=-1)
            cos = jnp.cos(idx_theta2)[None, :, None, :]
            sin = jnp.sin(idx_theta2)[None, :, None, :]
            neg_half = jnp.concatenate([-x[..., d2:], x[..., :d2]], axis=-1)
            return x * cos + neg_half * sin
        key = jax.random.key(seed)
        ks = jax.random.split(key, 6)
        s = 1.0 / np.sqrt(D_MODEL)
        return {'h': jax.random.normal(ks[0], (BATCH, SEQ, D_MODEL), jnp.float32), 'gamma': jnp.ones((D_MODEL,), jnp.float32), 'beta': jnp.zeros((D_MODEL,), jnp.float32), 'Wq': jax.random.normal(ks[1], (D_MODEL, N_HEADS * D_K), jnp.float32) * s, 'bq': jnp.zeros((N_HEADS * D_K,), jnp.float32), 'Wk': jax.random.normal(ks[2], (D_MODEL, N_HEADS * D_K), jnp.float32) * s, 'bk': jnp.zeros((N_HEADS * D_K,), jnp.float32), 'Wv': jax.random.normal(ks[3], (D_MODEL, N_HEADS * D_K), jnp.float32) * s, 'bv': jnp.zeros((N_HEADS * D_K,), jnp.float32), 'Wo': jax.random.normal(ks[4], (N_HEADS * D_K, D_MODEL), jnp.float32) * s, 'bo': jnp.zeros((D_MODEL,), jnp.float32)}
    _L0_attn_in = _L0_attn_setup()

    def _L0_ffn_setup():
        import jax, jax.numpy as jnp
        import numpy as np
        DIM = 256
        HIDDEN = 768
        SCALE = 1.0 / 127.0

        def _dequant(w_int, dtype):
            return w_int.astype(dtype) * jnp.asarray(SCALE, dtype)
        key = jax.random.key(seed)
        k_x, k_g, k_u, k_d = jax.random.split(key, 4)
        x = jax.random.normal(k_x, (4, 512, DIM), dtype=jnp.float32)
        w_gate = jax.random.randint(k_g, (HIDDEN, DIM), -127, 128, dtype=jnp.int32)
        w_up = jax.random.randint(k_u, (HIDDEN, DIM), -127, 128, dtype=jnp.int32)
        w_down = jax.random.randint(k_d, (DIM, HIDDEN), -127, 128, dtype=jnp.int32)
        return {'x': x, 'w_gate': w_gate, 'w_up': w_up, 'w_down': w_down}
    _L0_ffn_in = _L0_ffn_setup()
    _d = {'L0_attn_h': _L0_attn_in['h'], 'L0_attn_gamma': _L0_attn_in['gamma'], 'L0_attn_beta': _L0_attn_in['beta'], 'L0_attn_Wq': _L0_attn_in['Wq'], 'L0_attn_bq': _L0_attn_in['bq'], 'L0_attn_Wk': _L0_attn_in['Wk'], 'L0_attn_bk': _L0_attn_in['bk'], 'L0_attn_Wv': _L0_attn_in['Wv'], 'L0_attn_bv': _L0_attn_in['bv'], 'L0_attn_Wo': _L0_attn_in['Wo'], 'L0_attn_bo': _L0_attn_in['bo'], 'L0_ffn_w_gate': _L0_ffn_in['w_gate'], 'L0_ffn_w_up': _L0_ffn_in['w_up'], 'L0_ffn_w_down': _L0_ffn_in['w_down']}
    _x0 = _d['L0_attn_h']
    _d['L0_attn_h'] = jax.random.normal(jax.random.fold_in(jax.random.key(seed), 1), (2, 2048, 256), dtype=_x0.dtype)
    del _x0
    return _d

def reference(L0_attn_h, L0_attn_gamma, L0_attn_beta, L0_attn_Wq, L0_attn_bq, L0_attn_Wk, L0_attn_bk, L0_attn_Wv, L0_attn_bv, L0_attn_Wo, L0_attn_bo, L0_ffn_w_gate, L0_ffn_w_up, L0_ffn_w_down):

    def _L0_attn_ref(h, gamma, beta, Wq, bq, Wk, bk, Wv, bv, Wo, bo):
        import jax, jax.numpy as jnp
        import numpy as np
        D_MODEL = 256
        N_HEADS = 16
        D_K = 64
        SEQ = 1024
        BATCH = 1

        def _rope(x):
            d = x.shape[-1]
            d2 = d // 2
            theta = 1.0 / 10000.0 ** (jnp.arange(0, d, 2, dtype=jnp.float32) / d)
            pos = jnp.arange(x.shape[1], dtype=jnp.float32)
            idx_theta = pos[:, None] * theta[None, :]
            idx_theta2 = jnp.concatenate([idx_theta, idx_theta], axis=-1)
            cos = jnp.cos(idx_theta2)[None, :, None, :]
            sin = jnp.sin(idx_theta2)[None, :, None, :]
            neg_half = jnp.concatenate([-x[..., d2:], x[..., :d2]], axis=-1)
            return x * cos + neg_half * sin
        b, s, dm = h.shape
        h_res = h
        mu = jnp.mean(h, axis=-1, keepdims=True)
        var = jnp.var(h, axis=-1, keepdims=True)
        hn = (h - mu) * jax.lax.rsqrt(var + 1e-05) * gamma + beta
        mh = (b, s, N_HEADS, D_K)
        q = (hn @ Wq + bq).reshape(mh)
        k = (hn @ Wk + bk).reshape(mh)
        v = (hn @ Wv + bv).reshape(mh)
        q = _rope(q)
        k = _rope(k)
        scale = 1.0 / np.sqrt(D_K)
        attn = jnp.einsum('bihd,bjhd->bhij', q, k) * scale
        mask = jnp.tril(jnp.ones((s, s), dtype=bool))
        attn = jnp.where(mask, attn, -jnp.inf)
        attn = jax.nn.softmax(attn, axis=-1)
        out = jnp.einsum('bhij,bjhd->bihd', attn, v).reshape(b, s, N_HEADS * D_K)
        return out @ Wo + bo + h_res

    def _L0_ffn_ref(x, w_gate, w_up, w_down):
        import jax, jax.numpy as jnp
        import numpy as np
        DIM = 256
        HIDDEN = 768
        SCALE = 1.0 / 127.0

        def _dequant(w_int, dtype):
            return w_int.astype(dtype) * jnp.asarray(SCALE, dtype)
        wg = _dequant(w_gate, x.dtype)
        wu = _dequant(w_up, x.dtype)
        wd = _dequant(w_down, x.dtype)
        gate = jnp.einsum('bsd,hd->bsh', x, wg)
        up = jnp.einsum('bsd,hd->bsh', x, wu)
        h = jax.nn.silu(gate) * up
        return jnp.einsum('bsh,dh->bsd', h, wd)
    x = L0_attn_h
    x = _layernorm(x + _L0_attn_ref(x, L0_attn_gamma, L0_attn_beta, L0_attn_Wq, L0_attn_bq, L0_attn_Wk, L0_attn_bk, L0_attn_Wv, L0_attn_bv, L0_attn_Wo, L0_attn_bo), axis=-1)
    x = _layernorm(x + _L0_ffn_ref(x, L0_ffn_w_gate, L0_ffn_w_up, L0_ffn_w_down), axis=-1)
    return x

_drawn_inputs = setup_inputs


def setup_inputs(seed=0):
    import zlib

    import numpy as np

    out = dict(_drawn_inputs(seed))
    spreads = {'L0_attn_gamma': (1.0, 0.2),
     'L0_attn_beta': (0.0, 0.1),
     'L0_attn_bq': (0.0, 0.58),
     'L0_attn_bk': (0.0, 0.8),
     'L0_attn_bv': (0.0, 0.1),
     'L0_attn_bo': (0.0, 0.1)}
    factors = {}
    for name, (base, spread) in spreads.items():
        noise = np.random.default_rng([zlib.crc32(name.encode()), seed]).standard_normal(out[name].shape)
        drawn = base * np.exp(spread * noise) if base else spread * noise
        out[name] = jnp.asarray(drawn.astype(out[name].dtype))
    for name, factor in factors.items():
        out[name] = (out[name] * factor).astype(out[name].dtype)
    return out
```

```python
from contextlib import ExitStack

import concourse.bass as bass
from concourse import mybir

ALU = mybir.AluOpType
ACT = mybir.ActivationFunctionType
AX = mybir.AxisListType
F32 = mybir.dt.float32
F32R = mybir.dt.float32r
BF16 = mybir.dt.bfloat16
I32 = mybir.dt.int32

P = 128
BATCH, SEQ, DM = 2, 2048, 256
HEADS, DK = 16, 64
HID = 768
PAIRS = HEADS // 2
TT = SEQ // P
KC = DM // P
MC = HID // P
QKV = 3 * P
CH = 1024
TG = 4
GROUPS = TT // TG
OC = HEADS * DK // P
SCALE = DK ** -0.5
DEQ = 1.0 / 127.0
EPS = 1e-5
MASKED = -1e30


def postln_block_kernel(nc, h, gamma, beta, wqkv, bqkv, wo, bo, wgate_t, wup_t, wdown_t,
                        cos, sin, ident, ident2, mask, attn, out):
    with ExitStack() as ctx:
        def sb(name, shape, dt):
            return ctx.enter_context(nc.sbuf_tensor(name, shape, dt))

        def sem(name):
            return ctx.enter_context(nc.semaphore(name))

        hn = sb("hn", [P, 2, KC, SEQ], F32R)
        qk_hi = sb("qk_hi", [P, 4, SEQ], F32R)
        k_lo = sb("k_lo", [P, 2, SEQ], F32R)
        v_st = sb("v_st", [P, TT, 2, 2, DK], F32R)
        probs = sb("probs", [P, 2, SEQ], F32)
        pt_hi = sb("pt_hi", [P, 2, TT, 2 * P], F32R)
        pt_lo = sb("pt_lo", [P, 2, TT, 2 * P], F32R)
        o_norm = sb("o_norm", [P, TT, P], F32)
        w_hl = sb("w_hl", [P, 2, KC, QKV], F32R)
        b_raw = sb("b_raw", [DK, QKV], F32)
        b_hl = sb("b_hl", [DK, QKV], F32R)
        one_row = sb("one_row", [DK, P], F32R)
        cos_sb = sb("cos_sb", [P, TT, DK // 2], F32)
        sin_sb = sb("sin_sb", [P, TT, DK // 2], F32)
        nsin_sb = sb("nsin_sb", [P, TT, DK // 2], F32)
        id_f = sb("id_f", [P, P], F32)
        id_2 = sb("id_2", [P, DK], F32)
        id_b = sb("id_b", [P, P], BF16)
        mask_b = sb("mask_b", [P, P], BF16)
        o_sum = sb("o_sum", [P, 2, 2 * P], F32)
        gam = sb("gam", [P, KC], F32)
        bet = sb("bet", [P, KC], F32)
        bo_sb = sb("bo_sb", [P, DM], F32)
        stats = sb("stats", [P, TT, 6], F32)
        mv = sb("mv", [P, TT, 2], F32)
        std = sb("std", [P, TT], F32)
        rstd = sb("rstd", [P, TT], F32)
        nmax = sb("nmax", [P, 2, 2], F32)
        nmaxr = sb("nmaxr", [P, 2], F32)
        rsum = sb("rsum", [P, 32, 2], F32)
        rtot = sb("rtot", [P, 32], F32)
        pause = sb("pause", [P, 1], F32)
        rinv = sb("rinv", [P, 32], F32)

        pflat = probs[:, :, :].rearrange("p a n -> p (a n)")
        h_all = pflat.rearrange("p (t d) -> p t d", t=TT)
        qk_f = [pflat[:, 256 * i:256 * (i + 1)] for i in range(2)]
        rope_c = [pflat[:, 512 + 256 * i:768 + 256 * i] for i in range(2)]
        rope_s = [pflat[:, 1024 + 256 * i:1280 + 256 * i] for i in range(2)]
        rope_d = [pflat[:, 2048 + 512 * i:2560 + 512 * i] for i in range(2)]
        w_raw = pflat[:, 3072:3072 + KC * QKV].rearrange("p (k j n) -> p k j n", k=KC, j=3)
        onflat = o_norm[:, :, :].rearrange("p t d -> p (t d)")
        hn_f = [onflat[:, 512 * i:512 * (i + 1)] for i in range(2)]
        wo_raw = pflat[:, 0:OC * DM]
        wg_raw = pflat[:, OC * DM:OC * DM + KC * HID].bitcast(I32)
        wu_raw = pflat[:, 0:KC * HID].bitcast(I32)
        wd_raw = pflat[:, OC * DM:OC * DM + MC * DM].bitcast(I32)
        vflat = v_st[:, :, :, :, :].rearrange("p t a b d -> p (t a b d)")
        wo_hl = [vflat[:, OC * DM * i:OC * DM * (i + 1)] for i in range(2)]
        hnflat = hn[:, :, :, :].rearrange("p a k n -> p (a k n)")
        WG = KC * HID
        wg_hl = [hnflat[:, WG * i:WG * (i + 1)] for i in range(2)]
        wu_hl = [hnflat[:, WG * (2 + i):WG * (3 + i)] for i in range(2)]
        wd_hl = [hnflat[:, WG * 4:WG * 5],
                 w_hl[:, :, :, :].rearrange("p a k n -> p (a k n)")]
        o_all = pflat.rearrange("p (t n) -> p t n", t=TG)
        o_t = [x[:, :, :, :].rearrange("p a t q -> p (a t q)")[:, 0:OC * 512] for x in (pt_hi, pt_lo)]
        h_g = onflat[:, 0:TG * DM]
        x1_g = onflat[:, TG * DM:2 * TG * DM]
        klflat = k_lo[:, :, :].rearrange("p a n -> p (a n)")
        x1_t = [klflat[:, 1024 * i:1024 * (i + 1)] for i in range(2)]
        qkflat = qk_hi[:, :, :].rearrange("p a n -> p (a n)")
        hid_t = [qkflat[:, MC * 512 * i:MC * 512 * (i + 1)] for i in range(2)]
        silu_g = [pflat[:, 512 * i:512 * (i + 1)] for i in range(2)]
        hid_f = [pflat[:, 1024 + 512 * i:1536 + 512 * i] for i in range(2)]

        s_ps = ctx.enter_context(nc.psum_tensor("s_ps", [P, 2, CH], F32))
        t_ps = ctx.enter_context(nc.psum_tensor("t_ps", [P, 3, 512], F32))
        o_ps = ctx.enter_context(nc.psum_tensor("o_ps", [P, 512], F32))
        s_bank = [s_ps[:, i // 2, 512 * (i % 2):512 * (i % 2) + 512] for i in range(4)]
        y_ps = t_ps[:, 0:2, :].rearrange("p a n -> p (a n)")

        const_in = sem("const_in")
        primed = sem("primed")
        zeroed = sem("zeroed")
        ones_ready = sem("ones_ready")
        nsin_ready = sem("nsin_ready")
        h_in = sem("h_in")
        a_stats = sem("a_stats")
        a_aggr = sem("a_aggr")
        a_eps = sem("a_eps")
        a_std = sem("a_std")
        a_rstd = sem("a_rstd")
        a_norm = sem("a_norm")
        a_turned = sem("a_turned")
        a_affine = sem("a_affine")
        a_hi = sem("a_hi")
        a_lo = sem("a_lo")
        w_in = sem("w_in")
        w_hi = sem("w_hi")
        w_lo = sem("w_lo")
        qkv_done = sem("qkv_done")
        qk_copied = sem("qk_copied")
        v_hi = sem("v_hi")
        v_lo = sem("v_lo")
        roped_c = sem("roped_c")
        roped_s = sem("roped_s")
        roped = sem("roped")
        qk_turned = sem("qk_turned")
        qk_hi_done = sem("qk_hi_done")
        qk_lo_done = sem("qk_lo_done")
        scored = sem("scored")
        max_part = sem("max_part")
        maxed = sem("maxed")
        exped = sem("exped")
        turned = sem("turned")
        p_hi = sem("p_hi")
        p_lo = sem("p_lo")
        pv_done = sem("pv_done")
        o_out = sem("o_out")
        o_turned = sem("o_turned")
        r_sum = sem("r_sum")
        r_inv = sem("r_inv")
        normed = sem("normed")
        pair_done = sem("pair_done")
        o_stored = sem("o_stored")
        cw1_in = sem("cw1_in")
        cw2_in = sem("cw2_in")
        cw_hi = sem("cw_hi")
        cw_lo = sem("cw_lo")
        o_in = sem("o_in")
        c_turned = sem("c_turned")
        c_hi = sem("c_hi")
        c_lo = sem("c_lo")
        y_done = sem("y_done")
        ln_step = sem("ln_step")
        ln_stats = sem("ln_stats")
        ln_std = sem("ln_std")
        ln_rows = sem("ln_rows")
        x_turned = sem("x_turned")
        x_hi = sem("x_hi")
        x_lo = sem("x_lo")
        gate_up = sem("gate_up")
        silu_done = sem("silu_done")
        hid_done = sem("hid_done")
        hid_hi = sem("hid_hi")
        hid_lo = sem("hid_lo")
        z_done = sem("z_done")
        tile_done = sem("tile_done")
        out_stored = sem("out_stored")

        ROWS = 2 * TT

        def keys(r):
            return (r % TT + 1) * P

        chunks = [(r, c) for r in range(ROWS) for c in range(-(-keys(r) // CH))]
        chunk_no = {rc: i for i, rc in enumerate(chunks)}
        assert all(i % 2 == c for i, (r, c) in enumerate(chunks) if keys(r) > CH)
        groups = [(r, g) for r in range(ROWS) for g in range(-(-(r % TT + 1) // 4))]
        group_no = {rg: i for i, rg in enumerate(groups)}
        NCH, NG = len(chunks), len(groups)

        def row_chunks(r):
            return [rc for rc in chunks if rc[0] == r]

        def row_groups(r):
            return [rg for rg in groups if rg[0] == r]

        def groups_to(r):
            return sum(len(row_groups(i)) for i in range(r + 1))

        def steps():
            for r in range(ROWS + 3):
                tg = row_groups(r - 1) if 1 <= r <= ROWS else []
                q = (r - 3) // 2
                half = (r - 3) % 2
                yield (r,
                       r if r < ROWS else None,
                       (r - 5) // 2 if r >= 5 and r % 2 == 1 else None,
                       tg[0:2],
                       (q, half) if r >= 3 and q < ROWS // 2 else None,
                       tg[2:])

        ring = []
        for r, s, ot, t0, pv, t1 in steps():
            ring += [("turn", x) for x in t0]
            if ot is not None:
                ring.append(("out", ot))
            ring += [("turn", x) for x in t1]
        ring.append(("out", ROWS // 2 - 1))
        slot = {x: i for i, x in enumerate(ring)}

        def bank(x):
            return t_ps[:, slot[x] % 3, :]

        block = ctx.enter_context(nc.Block())

        @block.sync
        def _(sp):
            for dst, src in ((cos_sb[:, :, :], cos), (sin_sb[:, :, :], sin), (id_f[:, :], ident),
                             (id_2[:, :], ident2), (id_b[:, :], mask[0]), (mask_b[:, :], mask[1]),
                             (gam[:, :], gamma),
                             (bet[:, :], beta),
                             (bo_sb[:, :], bo.partition_broadcast(P))):
                sp.dma_start(dst, src).then_inc(const_in, 16)
            sp.wait_ge(primed, 1)
            with sp.Fori(0, BATCH) as b:
                sp.wait_ge(tile_done, b * GROUPS + 1)
                sp.dma_start(h_all, h[bass.ds(b, 1), :, :].rearrange("a (t p) d -> p (a t) d", p=P))\
                  .then_inc(h_in, 16)
                with sp.Fori(0, PAIRS) as pr:
                    it = b * PAIRS + pr
                    ready, end = sp.snap(it + 1), sp.snap(it + 2)
                    cols, turned_all = sp.snap(pr * P), sp.snap(b * (KC * GROUPS) + KC * GROUPS)
                    sp.wait_ge(a_turned, turned_all)
                    sp.wait_ge(pair_done, ready)
                    for j in range(3):
                        sp.dma_start(w_raw[:, :, j, :],
                                     wqkv[j, :, bass.ds(cols, P)].rearrange("(k p) n -> p k n", p=P))\
                          .then_inc(w_in, 16)
                    for j in range(3):
                        sp.dma_start(b_raw[:, j * P:(j + 1) * P],
                                     bqkv[j, bass.ds(cols, P)].partition_broadcast(DK)).then_inc(w_in, 16)
                    sp.wait_ge(pair_done, end)
                    sp.dma_start(attn[bass.ds(b, 1), :, bass.ds(cols, P)]
                                 .rearrange("a (t p) n -> p (a t) n", p=P), o_norm[:, :, :]).then_inc(o_stored, 16)
                sp.dma_start(wo_raw.rearrange("p (k n) -> p k n", k=OC),
                             wo.rearrange("(k p) n -> p k n", p=P)).then_inc(cw1_in, 16)
                sp.dma_start(wg_raw.rearrange("p (k n) -> p k n", k=KC),
                             wgate_t.rearrange("(k p) n -> p k n", p=P)).then_inc(cw1_in, 16)
                sp.wait_ge(cw_lo, b * 4 + 2)
                sp.dma_start(wu_raw.rearrange("p (k n) -> p k n", k=KC),
                             wup_t.rearrange("(k p) n -> p k n", p=P)).then_inc(cw2_in, 16)
                sp.dma_start(wd_raw.rearrange("p (k n) -> p k n", k=MC),
                             wdown_t.rearrange("(k p) n -> p k n", p=P)).then_inc(cw2_in, 16)
                with sp.Fori(0, GROUPS) as g:
                    c = b * GROUPS + g
                    weights, all_stored = sp.snap(b * 4 + 4), sp.snap(b * (16 * PAIRS) + (16 * PAIRS + 16))
                    sp.wait_ge(cw_lo, weights)
                    sp.wait_ge(o_stored, all_stored)
                    free, stored, done = sp.snap(c + 1), sp.snap(c * 16 + 16), sp.snap(c + 2)
                    rows = sp.snap(g * (TG * P))
                    sp.wait_ge(tile_done, free)
                    sp.wait_ge(out_stored, stored)
                    sp.dma_start(o_all, attn[bass.ds(b, 1), bass.ds(rows, TG * P), :]
                                 .rearrange("a (t p) n -> p (a t) n", p=P)).then_inc(o_in, 16)
                    sp.dma_start(h_g.rearrange("p (t d) -> p t d", t=TG),
                                 h[bass.ds(b, 1), bass.ds(rows, TG * P), :]
                                 .rearrange("a (t p) d -> p (a t) d", p=P)).then_inc(o_in, 16)
                    sp.wait_ge(tile_done, done)
                    sp.dma_start(out[bass.ds(b, 1), bass.ds(rows, TG * P), :]
                                 .rearrange("a (t p) d -> p (a t) d", p=P),
                                 h_g.rearrange("p (t d) -> p t d", t=TG)).then_inc(out_stored, 16)
            sp.wait_ge(out_stored, 16 * BATCH * GROUPS + 16)
            sp.wait_ge(o_stored, 16 * BATCH * PAIRS + 16)

        @block.gpsimd
        def _(pool):
            pool.wait_ge(const_in, 16 * 9)
            pool.wait_ge(nsin_ready, 1)
            with pool.Fori(0, BATCH * PAIRS) as it:
                for t in range(TT):
                    x = qk_f[t % 2].rearrange("p (v a d) -> p v a d", v=4, a=2)
                    o = rope_s[t % 2].rearrange("p (v a d) -> p v a d", v=4, a=2)
                    s = sin_sb[:, t, :].unsqueeze(1).broadcast_to([P, 4, DK // 2])
                    n = nsin_sb[:, t, :].unsqueeze(1).broadcast_to([P, 4, DK // 2])
                    pool.wait_ge(qk_copied, it * TT + (t + 1))
                    if t >= 2:
                        pool.wait_ge(roped, it * TT + (t - 1))
                    nc.gpsimd.tensor_tensor(o[:, :, 0, :], x[:, :, 1, :], n, ALU.mult).then_inc(roped_s, 1)
                    nc.gpsimd.tensor_tensor(o[:, :, 1, :], x[:, :, 0, :], s, ALU.mult).then_inc(roped_s, 1)

        @block.scalar
        def _(act):
            act.wait_ge(const_in, 16 * 9)
            nc.scalar.mul(nsin_sb[:, :, :], sin_sb[:, :, :], -1.0).then_inc(nsin_ready, 1)
            act.wait_ge(primed, 1)
            with act.Fori(0, BATCH) as b:
                act.wait_ge(out_stored, b * (16 * GROUPS) + 16)
                act.wait_ge(a_eps, b + 1)
                nc.scalar.activation(std[:, :], mv[:, :, 1], ACT.Sqrt).then_inc(a_std, 1)
                for i in range(KC * GROUPS):
                    k, g = i // GROUPS, i % GROUPS
                    act.wait_ge(a_turned, b * 8 + (i + 1))
                    if i >= 2:
                        act.wait_ge(a_lo, b * 8 + (i - 1))
                    nc.scalar.activation(hn_f[i % 2], s_bank[i % 4], ACT.Identity,
                                         bias=bet[:, k:k + 1], scale=gam[:, k:k + 1]).then_inc(a_affine, 1)
                    act.wait_ge(a_affine, b * 8 + (i + 1))
                    nc.scalar.activation(hn[:, 0, k, 512 * g:512 * (g + 1)], hn_f[i % 2], ACT.Copy)\
                      .then_inc(a_hi, 1)
                with act.Fori(0, PAIRS) as pr:
                    it = b * PAIRS + pr
                    act.wait_ge(w_in, it * 96 + 96)
                    wh = w_hl[:, 0, :, :].rearrange("p k (j n) -> p k j n", j=3)
                    nc.scalar.activation(wh[:, :, 0, :], w_raw[:, :, 0, :], ACT.Copy, scale=SCALE).then_inc(w_hi, 1)
                    nc.scalar.activation(w_hl[:, 0, :, P:QKV], w_raw[:, :, 1:3, :]
                                         .rearrange("p k j n -> p k (j n)"), ACT.Copy).then_inc(w_hi, 1)
                    nc.scalar.activation(b_hl[:, 0:P], b_raw[:, 0:P], ACT.Copy, scale=SCALE).then_inc(w_hi, 1)
                    nc.scalar.activation(b_hl[:, P:QKV], b_raw[:, P:QKV], ACT.Copy).then_inc(w_hi, 1)

                    def turned_hi(t):
                        act.wait_ge(qk_turned, it * TT + (t + 1))
                        nc.scalar.activation(qk_hi[:, :, t * P:(t + 1) * P],
                                             t_ps[:, t % 2, :].rearrange("p (v n) -> p v n", v=4), ACT.Copy)\
                          .then_inc(qk_hi_done, 1)

                    for t in range(TT + 2):
                        if t < TT:
                            act.wait_ge(qkv_done, it * TT + (t + 1))
                            if t >= 2:
                                act.wait_ge(roped_s, it * (2 * TT) + 2 * (t - 1))
                            nc.scalar.activation(qk_f[t % 2], s_bank[t % 2][:, 0:2 * P], ACT.Copy)\
                              .then_inc(qk_copied, 1)
                            nc.scalar.activation(v_st[:, t, :, 0, :],
                                                 s_bank[t % 2][:, 2 * P:3 * P]
                                                 .rearrange("p (a d) -> p a d", a=2), ACT.Copy).then_inc(v_hi, 1)
                        if t >= 2:
                            turned_hi(t - 2)

                    def hi_part(rg):
                        r, g = rg
                        n = min(4, r % TT + 1 - 4 * g)
                        if r >= 4:
                            act.wait_ge(pv_done, it * TT + (r // 2 - 1))
                        act.wait_ge(turned, it * NG + (group_no[rg] + 1))
                        nc.scalar.activation(
                            pt_hi[:, (r // 2) % 2, 4 * g:4 * g + n, (r % 2) * P:(r % 2 + 1) * P],
                            bank(("turn", rg))[:, 0:n * P].rearrange("p (k q) -> p k q", k=n), ACT.Copy)\
                          .then_inc(p_hi, 1)

                    def exp_part(rc):
                        r, c = rc
                        w = min(CH, keys(r) - c * CH)
                        act.wait_ge(maxed, it * ROWS + (r + 1))
                        if r >= 2 and c == 0:
                            act.wait_ge(turned, it * NG + groups_to(r - 2))
                        nc.scalar.activation(probs[:, r % 2, c * CH:c * CH + w],
                                             s_ps[:, chunk_no[rc] % 2, 0:w], ACT.Exp,
                                             bias=nmaxr[:, r % 2:r % 2 + 1], accum_out=rsum[:, r, c:c + 1])\
                          .then_inc(exped, 1)

                    for r, s, ot, t0, pv, t1 in steps():
                        for x in t0:
                            hi_part(x)
                        ex = row_chunks(s) if s is not None else []
                        for x in ex[0:1]:
                            exp_part(x)
                        for x in t1[0:1]:
                            hi_part(x)
                        for x in ex[1:2]:
                            exp_part(x)
                        for x in t1[1:]:
                            hi_part(x)
                        if pv is not None and pv[1] == 1:
                            q = pv[0]
                            act.wait_ge(pv_done, it * TT + (q + 1))
                            if q >= 2:
                                act.wait_ge(o_turned, it * TT + (q - 1))
                            nc.scalar.activation(o_sum[:, q % 2, :], o_ps[:, 0:2 * P], ACT.Copy).then_inc(o_out, 1)

                act.wait_ge(cw1_in, b * 32 + 32)
                nc.scalar.activation(wo_hl[0], wo_raw, ACT.Copy).then_inc(cw_hi, 1)
                nc.scalar.activation(wg_hl[0], wg_raw, ACT.Copy).then_inc(cw_hi, 1)
                act.wait_ge(cw2_in, b * 32 + 32)
                nc.scalar.activation(wu_hl[0], wu_raw, ACT.Copy).then_inc(cw_hi, 1)
                nc.scalar.activation(wd_hl[0], wd_raw, ACT.Copy).then_inc(cw_hi, 1)
                with act.Fori(0, GROUPS) as g:
                    c = b * GROUPS + g
                    for k in range(OC):
                        act.wait_ge(c_turned, c * OC + (k + 1))
                        nc.scalar.activation(o_t[0][:, 512 * k:512 * (k + 1)], s_bank[k % 4], ACT.Copy)\
                          .then_inc(c_hi, 1)
                    act.wait_ge(ln_step, c * 7 + 3)
                    nc.scalar.activation(std[:, 0:TG], mv[:, 0:TG, 1], ACT.Sqrt).then_inc(ln_std, 1)
                    for k in range(KC):
                        act.wait_ge(x_turned, c * KC + (k + 1))
                        nc.scalar.activation(x1_t[0][:, 512 * k:512 * (k + 1)], s_bank[k], ACT.Copy)\
                          .then_inc(x_hi, 1)
                    for m in range(MC + 1):
                        if m < MC:
                            act.wait_ge(gate_up, c * MC + (m + 1))
                            if m >= 2:
                                act.wait_ge(hid_done, c * MC + (m - 1))
                            nc.scalar.activation(silu_g[m % 2], s_bank[2 - 2 * (m % 2)], ACT.Silu, scale=DEQ)\
                              .then_inc(silu_done, 1)
                        if m >= 1:
                            act.wait_ge(hid_done, c * MC + m)
                            nc.scalar.activation(hid_t[0][:, 512 * (m - 1):512 * m], hid_f[(m - 1) % 2], ACT.Copy)\
                              .then_inc(hid_hi, 1)
                    act.wait_ge(ln_step, c * 7 + 6)
                    nc.scalar.activation(std[:, 0:TG], mv[:, 0:TG, 1], ACT.Sqrt).then_inc(ln_std, 1)

        @block.vector
        def _(dve):
            nc.vector.memset(one_row[:, :].bitcast(F32), 0.0).then_inc(zeroed, 1)
            dve.wait_ge(zeroed, 1)
            nc.vector.memset(one_row[0:1, :].bitcast(F32), 1.0).then_inc(ones_ready, 1)
            nc.vector.memset(one_row[32:33, :].bitcast(F32), 1.0).then_inc(ones_ready, 1)
            nc.vector.memset(rsum[:, :, :], 0.0).then_inc(ones_ready, 1)
            nc.vector.memset(nmaxr[:, 0:1], 0.0).then_inc(pair_done, 1)
            nc.vector.memset(nmaxr[:, 1:2], 0.0).then_inc(tile_done, 1)
            nc.vector.memset(rinv[:, :], 0.0).then_inc(out_stored, 16)
            nc.vector.memset(rtot[:, 0:16], 0.0).then_inc(o_stored, 16)
            nc.vector.memset(rtot[:, 16:32], 0.0).then_inc(primed, 1)
            with dve.Fori(0, BATCH) as b:
                dve.wait_ge(h_in, b * 16 + 16)
                for t in range(TT):
                    nc.vector.bn_stats(stats[:, t, :], h_all[:, t, :]).then_inc(a_stats, 1)
                dve.wait_ge(a_stats, b * TT + TT)
                nc.vector.memset(pause[:, :], 0.0).then_inc(a_aggr, 1)
                for t in range(TT):
                    nc.vector.bn_aggr(mv[:, t, :], stats[:, t, :]).then_inc(a_aggr, 1)
                dve.wait_ge(a_aggr, b * (TT + 1) + (TT + 1))
                nc.vector.tensor_scalar(mv[:, :, 1], mv[:, :, 1], EPS, None, ALU.add).then_inc(a_eps, 1)
                dve.wait_ge(a_std, b + 1)
                nc.vector.reciprocal(rstd[:, :], std[:, :]).then_inc(a_rstd, 1)
                dve.wait_ge(a_rstd, b + 1)
                for t in range(TT):
                    nc.vector.tensor_scalar(h_all[:, t, :], h_all[:, t, :], mv[:, t, 0:1], rstd[:, t:t + 1],
                                            ALU.subtract, ALU.mult).then_inc(a_norm, 1)
                for i in range(KC * GROUPS):
                    k, g = i // GROUPS, i % GROUPS
                    dve.wait_ge(a_hi, b * 8 + (i + 1))
                    nc.vector.tensor_tensor(hn[:, 1, k, 512 * g:512 * (g + 1)], hn_f[i % 2],
                                            hn[:, 0, k, 512 * g:512 * (g + 1)].bitcast(F32), ALU.subtract)\
                      .then_inc(a_lo, 1)
                with dve.Fori(0, PAIRS) as pr:
                    it = b * PAIRS + pr
                    dve.wait_ge(w_in, it * 96 + 96)
                    dve.wait_ge(w_hi, it * 4 + 4)
                    wv = w_hl[:, :, :, :].rearrange("p a k (j n) -> p a k j n", j=3)
                    nc.vector.scalar_tensor_tensor(
                        wv[:, 1, :, 0, :], w_raw[:, :, 0, :], SCALE, wv[:, 0, :, 0, :].bitcast(F32),
                        ALU.mult, ALU.subtract).then_inc(w_lo, 1)
                    nc.vector.tensor_tensor(
                        w_hl[:, 1, :, P:QKV], w_raw[:, :, 1:3, :].rearrange("p k j n -> p k (j n)"),
                        w_hl[:, 0, :, P:QKV].bitcast(F32), ALU.subtract).then_inc(w_lo, 1)
                    nc.vector.scalar_tensor_tensor(
                        b_hl[32:64, 0:P], b_raw[32:64, 0:P], SCALE, b_hl[32:64, 0:P].bitcast(F32),
                        ALU.mult, ALU.subtract).then_inc(w_lo, 1)
                    nc.vector.tensor_tensor(b_hl[32:64, P:QKV], b_raw[32:64, P:QKV],
                                            b_hl[32:64, P:QKV].bitcast(F32), ALU.subtract).then_inc(w_lo, 1)

                    def rope_sum(t):
                        dve.wait_ge(roped_c, it * TT + (t + 1))
                        dve.wait_ge(roped_s, it * (2 * TT) + 2 * (t + 1))
                        if t >= 2:
                            dve.wait_ge(qk_turned, it * TT + (t - 1))
                        twice = [x[t % 2].rearrange("p (v d) -> p v d", v=4).unsqueeze(2)
                                 .broadcast_to([P, 4, 2, DK]) for x in (rope_c, rope_s)]
                        nc.vector.tensor_tensor(rope_d[t % 2].rearrange("p (v a d) -> p v a d", v=4, a=2),
                                                *twice, ALU.add).then_inc(roped, 1)

                    def turned_lo(t):
                        dve.wait_ge(qk_hi_done, it * TT + (t + 1))
                        tp = t_ps[:, t % 2, :].rearrange("p (v n) -> p v n", v=4)
                        here = slice(t * P, (t + 1) * P)
                        nc.vector.tensor_tensor(k_lo[:, :, here], tp[:, 2:4, :],
                                                qk_hi[:, 2:4, here].bitcast(F32), ALU.subtract)\
                          .then_inc(qk_lo_done, 1)
                        nc.vector.tensor_tensor(qk_hi[DK:P, 0:2, here], tp[DK:P, 0:2, :],
                                                qk_hi[DK:P, 0:2, here].bitcast(F32), ALU.subtract)\
                          .then_inc(qk_lo_done, 1)

                    for t in range(TT + 2):
                        if t < TT:
                            dve.wait_ge(v_hi, it * TT + (t + 1))
                            if t >= 2:
                                dve.wait_ge(roped, it * TT + (t - 1))
                            nc.vector.tensor_tensor(
                                rope_c[t % 2].rearrange("p (v d) -> p v d", d=DK // 2),
                                s_bank[t % 2][:, 0:2 * P].rearrange("p (v d) -> p v d", d=DK // 2),
                                cos_sb[:, t, :].unsqueeze(1).broadcast_to([P, 8, DK // 2]), ALU.mult)\
                              .then_inc(roped_c, 1)
                            nc.vector.tensor_tensor(
                                v_st[:, t, :, 1, :],
                                s_bank[t % 2][:, 2 * P:3 * P].rearrange("p (a d) -> p a d", a=2),
                                v_st[:, t, :, 0, :].bitcast(F32), ALU.subtract).then_inc(v_lo, 1)
                        if 1 <= t <= TT:
                            rope_sum(t - 1)
                        if t >= 2:
                            turned_lo(t - 2)

                    def row_max(r):
                        rcs = row_chunks(r)
                        if r >= 2:
                            dve.wait_ge(exped, it * NCH + (chunk_no[row_chunks(r - 2)[-1]] + 1))
                        for _, c in rcs:
                            n = chunk_no[(r, c)]
                            w = min(CH, keys(r) - c * CH)
                            dve.wait_ge(scored, it * NCH + (n + 1))
                            dst = nmaxr[:, r % 2:r % 2 + 1] if len(rcs) == 1 else nmax[:, r % 2, c:c + 1]
                            last = nc.vector.tensor_reduce(dst, s_ps[:, n % 2, 0:w], AX.X, ALU.max, negate=True)
                            if len(rcs) > 1:
                                last.then_inc(max_part, 1)
                        if len(rcs) > 1:
                            dve.wait_ge(max_part, it * ROWS + 2 * ((r // TT) * (TT // 2) + r % TT - TT // 2 + 1))
                            last = nc.vector.tensor_tensor(nmaxr[:, r % 2:r % 2 + 1], nmax[:, r % 2, 0:1],
                                                           nmax[:, r % 2, 1:2], ALU.min)
                        last.then_inc(maxed, 1)

                    def lo_part(rg):
                        r, g = rg
                        n = min(4, r % TT + 1 - 4 * g)
                        dve.wait_ge(p_hi, it * NG + (group_no[rg] + 1))
                        here = (slice(None), (r // 2) % 2, slice(4 * g, 4 * g + n), slice((r % 2) * P, (r % 2 + 1) * P))
                        nc.vector.tensor_tensor(
                            pt_lo[here], bank(("turn", rg))[:, 0:n * P].rearrange("p (k q) -> p k q", k=n),
                            pt_hi[here].bitcast(F32), ALU.subtract).then_inc(p_lo, 1)

                    def divide(q):
                        rows = slice(2 * q, 2 * q + 2)
                        dve.wait_ge(o_turned, it * TT + (q + 1))
                        nc.vector.tensor_reduce(rtot[:, rows], rsum[:, rows, :], AX.X, ALU.add).then_inc(r_sum, 1)
                        dve.wait_ge(r_sum, it * TT + (q + 1))
                        nc.vector.reciprocal(rinv[:, rows], rtot[:, rows]).then_inc(r_inv, 1)
                        dve.wait_ge(r_inv, it * TT + (q + 1))
                        head = q // (TT // 2)
                        for a in range(2):
                            r = 2 * q + a
                            last = nc.vector.tensor_scalar(o_norm[:, r % TT, head * DK:(head + 1) * DK],
                                                           bank(("out", q))[:, a * DK:(a + 1) * DK],
                                                           rinv[:, r:r + 1], None, ALU.mult)
                            last.then_inc(normed, 1)

                    dve.wait_ge(o_stored, it * 16 + 16)
                    for r, s, ot, t0, pv, t1 in steps():
                        if s is not None:
                            row_max(s)
                        for x in t0:
                            lo_part(x)
                        if ot is not None:
                            divide(ot)
                        for x in t1:
                            lo_part(x)
                    divide(ROWS // 2 - 1)
                    dve.wait_ge(normed, it * ROWS + ROWS)
                    nc.vector.memset(rtot[:, 0:1], 0.0).then_inc(pair_done, 1)

                def split(n, dst, raw, src):
                    dve.wait_ge(cw_hi, b * 4 + (n + 1))
                    nc.vector.tensor_tensor(dst[1], raw, dst[0].bitcast(F32), ALU.subtract).then_inc(cw_lo, 1)

                split(0, wo_hl, wo_raw, cw1_in)
                split(1, wg_hl, wg_raw, cw1_in)
                split(2, wu_hl, wu_raw, cw2_in)
                split(3, wd_hl, wd_raw, cw2_in)
                with dve.Fori(0, GROUPS) as g:
                    c = b * GROUPS + g
                    for k in range(OC):
                        dve.wait_ge(c_hi, c * OC + (k + 1))
                        nc.vector.tensor_tensor(o_t[1][:, 512 * k:512 * (k + 1)], s_bank[k % 4],
                                                o_t[0][:, 512 * k:512 * (k + 1)].bitcast(F32), ALU.subtract)\
                          .then_inc(c_lo, 1)

                    def step(ins, n):
                        ins.then_inc(ln_step, 1)
                        dve.wait_ge(ln_step, c * 7 + n)

                    def norm(x, n, second):
                        for t in range(TG):
                            last = nc.vector.bn_stats(stats[:, t, :], x[:, t * DM:(t + 1) * DM])
                            last.then_inc(ln_stats, 1)
                        dve.wait_ge(ln_stats, c * (4 * TG + 2) + second * (2 * TG + 1) + TG)
                        nc.vector.memset(pause[:, :], 0.0).then_inc(ln_stats, 1)
                        for t in range(TG):
                            last = nc.vector.bn_aggr(mv[:, t, :], stats[:, t, :])
                            last.then_inc(ln_stats, 1)
                        dve.wait_ge(ln_stats, c * (4 * TG + 2) + (second + 1) * (2 * TG + 1))
                        step(nc.vector.tensor_scalar(mv[:, 0:TG, 1], mv[:, 0:TG, 1], EPS, None, ALU.add), n + 1)
                        dve.wait_ge(ln_std, c * 2 + (second + 1))
                        step(nc.vector.reciprocal(rstd[:, 0:TG], std[:, 0:TG]), n + 2)
                        for t in range(TG):
                            last = nc.vector.tensor_scalar(x[:, t * DM:(t + 1) * DM], x[:, t * DM:(t + 1) * DM],
                                                           mv[:, t, 0:1], rstd[:, t:t + 1],
                                                           ALU.subtract, ALU.mult)
                            last.then_inc(ln_rows, 1)

                    dve.wait_ge(o_in, c * 32 + 32)
                    dve.wait_ge(y_done, c + 1)
                    step(nc.vector.scalar_tensor_tensor(x1_g, h_g, 2.0, y_ps, ALU.mult, ALU.add), 1)
                    x3 = x1_g.rearrange("p (t d) -> p t d", t=TG)
                    step(nc.vector.tensor_tensor(x3, x3, bo_sb[:, :].unsqueeze(1).broadcast_to([P, TG, DM]),
                                                 ALU.add), 2)
                    norm(x1_g, 2, 0)
                    for k in range(KC):
                        dve.wait_ge(x_hi, c * KC + (k + 1))
                        nc.vector.tensor_tensor(x1_t[1][:, 512 * k:512 * (k + 1)], s_bank[k],
                                                x1_t[0][:, 512 * k:512 * (k + 1)].bitcast(F32), ALU.subtract)\
                          .then_inc(x_lo, 1)
                    for m in range(MC + 1):
                        if m < MC:
                            dve.wait_ge(silu_done, c * MC + (m + 1))
                            if m >= 2:
                                dve.wait_ge(hid_hi, c * MC + (m - 1))
                                dve.wait_ge(hid_lo, c * MC + (m - 1))
                            nc.vector.scalar_tensor_tensor(hid_f[m % 2], s_bank[3 - 2 * (m % 2)], DEQ, silu_g[m % 2],
                                                           ALU.mult, ALU.mult).then_inc(hid_done, 1)
                        if m >= 1:
                            dve.wait_ge(hid_hi, c * MC + m)
                            nc.vector.tensor_tensor(hid_t[1][:, 512 * (m - 1):512 * m], hid_f[(m - 1) % 2],
                                                    hid_t[0][:, 512 * (m - 1):512 * m].bitcast(F32), ALU.subtract)\
                              .then_inc(hid_lo, 1)
                    dve.wait_ge(z_done, c + 1)
                    dve.wait_ge(ln_rows, c * (2 * TG) + TG)
                    step(nc.vector.scalar_tensor_tensor(h_g, y_ps, DEQ, x1_g, ALU.mult, ALU.add), 5)
                    norm(h_g, 5, 1)
                    dve.wait_ge(ln_rows, c * (2 * TG) + 2 * TG)
                    nc.vector.memset(rtot[:, 0:1], 0.0).then_inc(tile_done, 1)

        @block.tensor
        def _(pe):
            def product(dst, lhs, rhs, first=True, last=True):
                nc.tensor.matmul(dst, lhs[0], rhs[0], start=first, stop=False)
                nc.tensor.matmul(dst, lhs[1], rhs[0], start=False, stop=False)
                return nc.tensor.matmul(dst, lhs[0], rhs[1], start=False, stop=last)

            pe.wait_ge(const_in, 16 * 9)
            pe.wait_ge(ones_ready, 3)
            pe.wait_ge(primed, 1)
            with pe.Fori(0, BATCH) as b:
                for i in range(KC * GROUPS):
                    k, g = i // GROUPS, i % GROUPS
                    if k == 0:
                        pe.wait_ge(a_norm, b * TT + 4 * (g + 1))
                    if i >= 4:
                        pe.wait_ge(a_affine, b * 8 + (i - 3))
                    for j in range(4):
                        last = nc.tensor.transpose(s_bank[i % 4][:, j * P:(j + 1) * P],
                                                   h_all[:, 4 * g + j, k * P:(k + 1) * P], id_f[:, :])
                    last.then_inc(a_turned, 1)
                with pe.Fori(0, PAIRS) as pr:
                    it = b * PAIRS + pr
                    pe.wait_ge(a_lo, b * 8 + 8)
                    pe.wait_ge(pair_done, it + 1)
                    pe.wait_ge(w_lo, it * 4 + 4)

                    def turn(t):
                        pe.wait_ge(roped, it * TT + (t + 1))
                        if t >= 2:
                            pe.wait_ge(qk_lo_done, it * (2 * TT) + 2 * (t - 1))
                        for v in range(4):
                            last = nc.tensor.transpose(t_ps[:, t % 2, v * P:(v + 1) * P],
                                                       rope_d[t % 2][:, v * P:(v + 1) * P], id_f[:, :])
                        last.then_inc(qk_turned, 1)

                    for t in range(TT + 2):
                        if t < TT:
                            if t >= 2:
                                pe.wait_ge(v_lo, it * TT + (t - 1))
                            dst = s_bank[t % 2][:, 0:QKV]
                            here = slice(t * P, (t + 1) * P)
                            for k in range(KC):
                                product(dst, [hn[:, a, k, here] for a in range(2)],
                                        [w_hl[:, a, k, :] for a in range(2)], first=(k == 0), last=False)
                            nc.tensor.matmul(dst, one_row[:, :], b_hl[:, :], start=False, stop=True)\
                              .then_inc(qkv_done, 1)
                        if t >= 2:
                            turn(t - 2)

                    pe.wait_ge(qk_lo_done, it * (2 * TT) + 2 * TT)
                    pe.wait_ge(v_lo, it * TT + TT)

                    def scores(r):
                        head, t = r // TT, r % TT
                        q = qk_hi[:, head, t * P:(t + 1) * P]
                        for _, c in row_chunks(r):
                            n = chunk_no[(r, c)]
                            if n >= 2:
                                pe.wait_ge(exped, it * NCH + (n - 1))
                            end = min((c + 1) * CH, keys(r))
                            for k0 in range(c * CH, end, 512):
                                k1 = min(k0 + 512, end)
                                dst = s_ps[:, n % 2, k0 - c * CH:k1 - c * CH]
                                diag = k1 == keys(r)
                                nc.tensor.matmul(dst, q, qk_hi[:, 2 + head, k0:k1], start=True, stop=False)
                                last = nc.tensor.matmul(dst, q, k_lo[:, head, k0:k1], start=False, stop=not diag)
                                if diag:
                                    w = k1 - c * CH
                                    last = nc.tensor.matmul(s_ps[:, n % 2, w - P:w], id_b[:, :], mask_b[:, :],
                                                            start=False, stop=True)
                            last.then_inc(scored, 1)

                    def ring_free(x):
                        u = slot[x] - 3
                        if u >= 0:
                            kind, y = ring[u]
                            if kind == "turn":
                                pe.wait_ge(p_lo, it * NG + (group_no[y] + 1))
                            else:
                                pe.wait_ge(normed, it * ROWS + 2 * (y + 1))

                    def turn_probs(rg):
                        r, g = rg
                        ring_free(("turn", rg))
                        if g == 0:
                            pe.wait_ge(exped, it * NCH + (chunk_no[row_chunks(r)[-1]] + 1))
                        for k in range(4 * g, min(4 * g + 4, r % TT + 1)):
                            last = nc.tensor.transpose(bank(("turn", rg))[:, (k - 4 * g) * P:(k - 4 * g + 1) * P],
                                                       probs[:, r % 2, k * P:(k + 1) * P], id_f[:, :])
                        last.then_inc(turned, 1)

                    def pv_part(q, half):
                        head, n = q // (TT // 2), 2 * (q % (TT // 2)) + 2
                        if half == 0:
                            pe.wait_ge(p_lo, it * NG + groups_to(2 * q + 1))
                            if q >= 1:
                                pe.wait_ge(o_out, it * TT + q)
                        for k in range(half * n // 2, (half + 1) * n // 2):
                            c0 = P if k == n - 1 else 0
                            v = v_st[:, k, head, :, :].rearrange("p a d -> p (a d)")
                            for part in (pt_hi, pt_lo):
                                last = nc.tensor.matmul(o_ps[:, c0:2 * P], v, part[:, q % 2, k, c0:2 * P],
                                                        start=(k == 0 and part is pt_hi),
                                                        stop=(k == n - 1 and part is pt_lo),
                                                        skip_group_check=True)
                        if half == 1:
                            last.then_inc(pv_done, 1)

                    def turn_out(q):
                        ring_free(("out", q))
                        pe.wait_ge(o_out, it * TT + (q + 1))
                        for a in range(2):
                            last = nc.tensor.matmul(bank(("out", q))[:, a * DK:(a + 1) * DK],
                                                    o_sum[:, q % 2, a * P:(a + 1) * P], id_2[:, :],
                                                    start=True, stop=True)
                        last.then_inc(o_turned, 1)

                    for r, s, ot, t0, pv, t1 in steps():
                        if s is not None:
                            scores(s)
                        for x in t0:
                            turn_probs(x)
                        if ot is not None:
                            turn_out(ot)
                        if pv is not None:
                            pv_part(*pv)
                        for x in t1:
                            turn_probs(x)
                    turn_out(ROWS // 2 - 1)

                with pe.Fori(0, GROUPS) as g:
                    c = b * GROUPS + g
                    pe.wait_ge(cw_lo, b * 4 + 4)
                    pe.wait_ge(o_in, c * 32 + 32)
                    for k in range(OC):
                        if k >= 4:
                            pe.wait_ge(c_lo, c * OC + (k - 3))
                        for t in range(TG):
                            last = nc.tensor.transpose(s_bank[k % 4][:, t * P:(t + 1) * P],
                                                       o_all[:, t, k * P:(k + 1) * P], id_f[:, :])
                        last.then_inc(c_turned, 1)
                    pe.wait_ge(c_lo, c * OC + OC)
                    for t in range(TG):
                        for k in range(OC):
                            last = product(y_ps[:, t * DM:(t + 1) * DM],
                                           [x[:, 512 * k + t * P:512 * k + (t + 1) * P] for x in o_t],
                                           [x[:, k * DM:(k + 1) * DM] for x in wo_hl],
                                           first=(k == 0), last=(k == OC - 1))
                    last.then_inc(y_done, 1)
                    pe.wait_ge(ln_rows, c * (2 * TG) + TG)
                    for k in range(KC):
                        for t in range(TG):
                            last = nc.tensor.transpose(s_bank[k][:, t * P:(t + 1) * P],
                                                       x1_g[:, t * DM + k * P:t * DM + (k + 1) * P], id_f[:, :])
                        last.then_inc(x_turned, 1)
                    pe.wait_ge(x_lo, c * KC + KC)
                    for m in range(MC):
                        if m >= 2:
                            pe.wait_ge(hid_done, c * MC + (m - 1))
                        for dst, w in ((s_bank[2 - 2 * (m % 2)], wg_hl), (s_bank[3 - 2 * (m % 2)], wu_hl)):
                            for k in range(KC):
                                last = product(dst, [x[:, k * HID + m * P:k * HID + (m + 1) * P] for x in w],
                                               [x[:, 512 * k:512 * (k + 1)] for x in x1_t],
                                               first=(k == 0), last=(k == KC - 1))
                        last.then_inc(gate_up, 1)
                    pe.wait_ge(hid_lo, c * MC + MC)
                    for t in range(TG):
                        for m in range(MC):
                            last = product(y_ps[:, t * DM:(t + 1) * DM],
                                           [x[:, 512 * m + t * P:512 * m + (t + 1) * P] for x in hid_t],
                                           [x[:, m * DM:(m + 1) * DM] for x in wd_hl],
                                           first=(m == 0), last=(m == MC - 1))
                    last.then_inc(z_done, 1)


_INS = ["h", "gamma", "beta", "wqkv", "bqkv", "wo", "bo", "wgate_t", "wup_t", "wdown_t",
        "cos", "sin", "ident", "ident2", "mask"]


def kernel(L0_attn_h, L0_attn_gamma, L0_attn_beta, L0_attn_Wq, L0_attn_bq, L0_attn_Wk, L0_attn_bk,
           L0_attn_Wv, L0_attn_bv, L0_attn_Wo, L0_attn_bo, L0_ffn_w_gate, L0_ffn_w_up, L0_ffn_w_down):
    import ml_dtypes
    import numpy as np
    import concourse.bacc as bacc
    from concourse.bass_utils import run_bass_kernel_spmd

    theta = np.float32(1.0) / np.float32(10000.0) ** (np.arange(0, DK, 2, dtype=np.float32) / np.float32(DK))
    angle = np.arange(SEQ, dtype=np.float32)[:, None] * theta[None, :].astype(np.float32)
    tiled = angle.reshape(TT, P, DK // 2).transpose(1, 0, 2)
    eye = np.eye(P, dtype=np.float32)
    later = np.triu(np.full((P, P), MASKED, np.float32), 1)

    arrays = {
        "h": L0_attn_h, "gamma": np.reshape(L0_attn_gamma, (KC, P)).T, "beta": np.reshape(L0_attn_beta, (KC, P)).T,
        "wqkv": np.stack([L0_attn_Wq, L0_attn_Wk, L0_attn_Wv]),
        "bqkv": np.stack([L0_attn_bq, L0_attn_bk, L0_attn_bv]),
        "wo": L0_attn_Wo, "bo": L0_attn_bo,
        "wgate_t": np.transpose(L0_ffn_w_gate), "wup_t": np.transpose(L0_ffn_w_up),
        "wdown_t": np.transpose(L0_ffn_w_down),
        "cos": np.cos(tiled).astype(np.float32), "sin": np.sin(tiled).astype(np.float32),
        "ident": eye, "ident2": np.concatenate([eye[:DK, :DK]] * 2),
        "mask": np.stack([eye, later]).astype(ml_dtypes.bfloat16),
    }
    arrays = {n: np.ascontiguousarray(a) for n, a in arrays.items()}
    nc = bacc.Bacc("TRN2", target_bir_lowering=False, num_devices=1)
    args = [nc.dram_tensor(f"in_{n}", arrays[n].shape, mybir.dt.from_np(arrays[n].dtype),
                           kind="ExternalInput").ap() for n in _INS]
    attn = nc.dram_tensor("attn", (BATCH, SEQ, HEADS * DK), F32, kind="Internal").ap()
    out = nc.dram_tensor("out", (BATCH, SEQ, DM), F32, kind="ExternalOutput").ap()
    postln_block_kernel(nc, *args, attn, out)
    r = run_bass_kernel_spmd(nc, [{f"in_{n}": arrays[n] for n in _INS}], core_ids=[0])
    return r.results[0]["out"]
```

```python
from contextlib import ExitStack

import concourse.bass as bass
from concourse import mybir

ALU = mybir.AluOpType
ACT = mybir.ActivationFunctionType
AX = mybir.AxisListType
F32 = mybir.dt.float32
F32R = mybir.dt.float32r
BF16 = mybir.dt.bfloat16
I32 = mybir.dt.int32

P = 128
BATCH, SEQ, DM = 2, 2048, 256
HEADS, DK = 16, 64
HID = 768
PAIRS = HEADS // 2
TT = SEQ // P
KC = DM // P
MC = HID // P
QKV = 3 * P
TG = 4
GROUPS = TT // TG
OC = HEADS * DK // P
SCALE = DK ** -0.5
DEQ = 1.0 / 127.0
EPS = 1e-5
MASKED = -1e30
ROWS = 2 * TT
COUPLES = ROWS // 2


def postln_block_kernel(nc, h, gamma, beta, wqkv, bqkv, wo, bo, wgate_t, wup_t, wdown_t,
                        cos, sin, ident, ident2, mask, attn, out):
    with ExitStack() as ctx:
        def sb(name, shape, dt):
            return ctx.enter_context(nc.sbuf_tensor(name, shape, dt))

        def sem(name):
            return ctx.enter_context(nc.semaphore(name))

        cos_sb = sb("cos_sb", [P, TT, DK // 2], F32)
        sin_sb = sb("sin_sb", [P, TT, DK // 2], F32)
        id_f = sb("id_f", [P, P], F32)
        id_2 = sb("id_2", [P, DK], F32)
        id_b = sb("id_b", [P, P], BF16)
        mask_b = sb("mask_b", [P, P], BF16)
        gam = sb("gam", [P, KC], F32)
        bet = sb("bet", [P, KC], F32)
        stats = sb("stats", [P, TT, 6], F32)
        mv = sb("mv", [P, TT, 2], F32)
        std = sb("std", [P, TT], F32)
        rstd = sb("rstd", [P, TT], F32)
        nmax_part = sb("nmax_part", [P, 2, 4], F32)
        nmax = sb("nmax", [P, 2], F32)
        rsum = sb("rsum", [P, ROWS, 4], F32)
        rtot = sb("rtot", [P, ROWS], F32)
        rinv = sb("rinv", [P, ROWS], F32)
        pause = sb("pause", [P, 1], F32)

        with ExitStack() as ctx_attn:
            def sba(name, shape, dt):
                return ctx_attn.enter_context(nc.sbuf_tensor(name, shape, dt))

            hn = sba("hn", [P, 2, KC, SEQ], F32R)
            qk_hi = sba("qk_hi", [P, 4, SEQ], F32R)
            k_lo = sba("k_lo", [P, 2, SEQ], F32R)
            v_st = sba("v_st", [P, TT, 2, 2, DK], F32R)
            pt_hi = sba("pt_hi", [P, 2, TT, 2 * P], F32R)
            pt_lo = sba("pt_lo", [P, 2, TT, 2 * P], F32R)
            o_norm = sba("o_norm", [P, TT, P], F32)
            o_sum = sba("o_sum", [P, 2 * P], F32)
            w_hl = sba("w_hl", [P, 2, KC, QKV], F32R)
            w_raw = sba("w_raw", [P, KC, 3, P], F32)
            b_qkv = sba("b_qkv", [P, 3, P], F32)
            qkv_f = [sba(f"qkv_f{i}", [P, 3, DK], F32) for i in range(4)]
            rope_s = sba("rope_s", [P, 2, DK], F32)
            rope_d = [sba(f"rope_d{i}", [P, 2, 2, DK], F32) for i in range(2)]
            probs = sba("probs", [P, 2, SEQ], F32)

        pflat = probs[:, :, :].rearrange("p a n -> p (a n)")
        h_all = pflat.rearrange("p (t d) -> p t d", t=TT)
        onflat = o_norm[:, :, :].rearrange("p t d -> p (t d)")
        hn_f = [onflat[:, 512 * i:512 * (i + 1)] for i in range(2)]

        def split_sb(name, n):
            t = sb(name, [P, 2, n], F32R)
            return [t[:, 0, :], t[:, 1, :]]

        wo_raw = sb("wo_raw", [P, OC * DM], F32)[:, :]
        wg_raw = sb("wg_raw", [P, KC * HID], I32)[:, :]
        wu_raw = sb("wu_raw", [P, KC * HID], I32)[:, :]
        wd_raw = sb("wd_raw", [P, MC * DM], I32)[:, :]
        bo_sb = sb("bo_sb", [P, DM], F32)
        h_g = sb("h_g", [P, TG * DM], F32)[:, :]

        wo_hl = split_sb("wo_hl", OC * DM)
        wg_hl = split_sb("wg_hl", KC * HID)
        wu_hl = split_sb("wu_hl", KC * HID)
        wd_hl = split_sb("wd_hl", MC * DM)

        o_t = split_sb("o_t", OC * 512)
        x1_t = split_sb("x1_t", KC * 512)
        hid_t = split_sb("hid_t", MC * 512)
        o_all = sb("o_all", [P, TG, HEADS * DK], F32)[:, :, :]
        x1_g = sb("x1_g", [P, TG * DM], F32)[:, :]
        x1_keep = sb("x1_keep", [P, TG * DM], F32)[:, :]
        out_g = sb("out_g", [P, TG * DM], F32)[:, :]
        silu_g = [sb(f"silu_g{i}", [P, 512], F32)[:, :] for i in range(2)]
        hid_f = [sb(f"hid_f{i}", [P, 512], F32)[:, :] for i in range(2)]

        with ExitStack() as ctx_ps:
            s_ps = ctx_ps.enter_context(nc.psum_tensor("s_ps", [P, 4, 512], F32))
            t_ps = ctx_ps.enter_context(nc.psum_tensor("t_ps", [P, 3, 512], F32))
            o_ps = ctx_ps.enter_context(nc.psum_tensor("o_ps", [P, 512], F32))
        s_bank = [s_ps[:, i, :] for i in range(4)]
        gu_ps = ctx.enter_context(nc.psum_tensor("gu_ps", [P, 4, 512], F32))
        y_ps = ctx.enter_context(nc.psum_tensor("y_ps", [P, TG * DM], F32))[:, :]
        z_ps = ctx.enter_context(nc.psum_tensor("z_ps", [P, TG * DM], F32))[:, :]
        gu_bank = [gu_ps[:, i, :] for i in range(4)]

        const_in = sem("const_in")
        primed = sem("primed")
        ones_ready = sem("ones_ready")
        h_in = sem("h_in")
        a_stats = sem("a_stats")
        a_aggr = sem("a_aggr")
        a_eps = sem("a_eps")
        a_std = sem("a_std")
        a_rstd = sem("a_rstd")
        a_norm = sem("a_norm")
        a_turned = sem("a_turned")
        a_affine = sem("a_affine")
        a_hi = sem("a_hi")
        a_lo = sem("a_lo")
        w_in = sem("w_in")
        w_hi = sem("w_hi")
        w_lo = sem("w_lo")
        qkv_done = sem("qkv_done")
        qkv_copied = sem("qkv_copied")
        v_hi = sem("v_hi")
        v_lo = sem("v_lo")
        biased = sem("biased")
        rope_mul = sem("rope_mul")
        roped = sem("roped")
        b_scaled = sem("b_scaled")
        b_in = [sem(f"b_in{i}") for i in range(2)]
        qk_turned = sem("qk_turned")
        qk_hi_done = sem("qk_hi_done")
        qk_lo_done = sem("qk_lo_done")
        scored = sem("scored")
        max_part = sem("max_part")
        maxed = sem("maxed")
        exped = sem("exped")
        turned = sem("turned")
        p_hi = sem("p_hi")
        p_lo = sem("p_lo")
        pv_done = sem("pv_done")
        o_out = sem("o_out")
        o_turned = sem("o_turned")
        r_sum = sem("r_sum")
        r_inv = sem("r_inv")
        normed = sem("normed")
        o_stored = [sem(f"o_stored{i}") for i in range(2)]
        cw_in = sem("cw_in")
        bo_in = sem("bo_in")
        hg_in = sem("hg_in")
        x_added = sem("x_added")
        x_kept = sem("x_kept")
        z_added = sem("z_added")
        cw_hi = sem("cw_hi")
        cw_lo = sem("cw_lo")
        o_in = sem("o_in")
        c_turned = sem("c_turned")
        c_hi = sem("c_hi")
        c_lo = sem("c_lo")
        y_done = sem("y_done")
        ln_eps = sem("ln_eps")
        ln_rstd = sem("ln_rstd")
        x_biased = sem("x_biased")
        out_rows = sem("out_rows")
        ln_stats = sem("ln_stats")
        ln_std = sem("ln_std")
        ln_rows = sem("ln_rows")
        x_turned = sem("x_turned")
        x_hi = sem("x_hi")
        x_lo = sem("x_lo")
        gate_up = sem("gate_up")
        silu_done = sem("silu_done")
        hid_done = sem("hid_done")
        hid_hi = sem("hid_hi")
        hid_lo = sem("hid_lo")
        z_done = sem("z_done")
        tile_done = sem("tile_done")
        out_stored = sem("out_stored")

        MUL, TURN_QK, EXP, TURN, PV, FIN = 4, 2, -1, -2, -4, -6
        order = [(0, t) for t in range(TT)] + [(1, t) for t in range(TT)]

        def row(j):
            return order[j % ROWS]

        def row_units(j):
            return [(j, u) for u in range(row(j)[1] // 4 + 1)]

        def width(x):
            return min(4, row(x[0])[1] + 1 - 4 * x[1])

        NU = sum(len(row_units(j)) for j in range(ROWS))
        assert NU % 4 == 0

        def units_to(j):
            return NU * (j // ROWS) + sum(len(row_units(a)) for a in range(j % ROWS + 1))

        def unit_no(x):
            return units_to(x[0] - 1) + x[1]

        NPART = sum(len(row_units(j)) for j in range(ROWS) if len(row_units(j)) > 1)

        def parts_to(j):
            return NPART * (j // ROWS) + sum(len(row_units(a)) for a in range(j % ROWS + 1)
                                             if len(row_units(a)) > 1)

        class Steps:
            def __init__(self, kind):
                self.rows = range(0 if kind == "first" else -ROWS, ROWS if kind == "last" else 2 * ROWS)
                self.steps = range(-MUL if kind == "first" else 0, ROWS - FIN if kind == "last" else ROWS)

            def tile(self, i, stage):
                return [i + stage] if i + stage in self.rows else []

            def units(self, i, stage):
                return row_units(i + stage) if i + stage in self.rows else []

            def couple(self, i, stage):
                return [(i + stage) // 2] if i + stage in self.rows else []

            def final(self, i):
                return self.couple(i, FIN) if i % 2 == 0 else []

        WEIGHTS_A, WEIGHTS_B, BIAS_A, BIAS_B = TT - 2, 2 * TT - 4, TT + 4, 4

        FIRST, MIDDLE, LAST = Steps("first"), Steps("middle"), Steps("last")

        ring = []
        for i in range(ROWS):
            tr = [("turn",) + x for x in MIDDLE.units(i, TURN)]
            ring += tr[0:1] + [("out", 2 * c, 0) for c in MIDDLE.final(i)] + [("mul", i + MUL, 0)]
            ring += tr[1:2] + [("qk", i + TURN_QK, 0)] + tr[2:4]
        while len(ring) % 3:
            ring.append(None)
        slots = {x: n for n, x in enumerate(ring) if x}
        ring_step = {"turn": -TURN, "out": -FIN, "mul": -MUL, "qk": -TURN_QK}

        def slot(x):
            kind, j, u = x
            pairs = (j + ring_step[kind]) // ROWS
            return slots[(kind, j - pairs * ROWS, u)] + pairs * len(ring)

        def bank(kind, j, u=0):
            return t_ps[:, slot((kind, j, u)) % 3, :]

        def use_before(seq, x):
            n = slot(x) - 3
            while True:
                pairs, y = n // len(ring), ring[n % len(ring)]
                if y is not None:
                    y = (y[0], y[1] + pairs * ROWS, y[2])
                    if y[1] in seq.rows:
                        return y
                    if y[1] + ring_step[y[0]] < seq.steps[0]:
                        return None
                n -= 3

        block = ctx.enter_context(nc.Block())

        @block.sync
        def _(sp):
            for dst, src in ((cos_sb[:, :, :], cos), (sin_sb[:, :, :], sin), (id_f[:, :], ident),
                             (id_2[:, :], ident2), (id_b[:, :], mask[0]), (mask_b[:, :], mask[1]),
                             (gam[:, :], gamma),
                             (bet[:, :], beta)):
                sp.dma_start(dst, src).then_inc(const_in, 16)
            sp.wait_ge(primed, 1)
            with sp.Fori(0, BATCH) as b:
                sp.wait_ge(tile_done, b * GROUPS + 1)
                sp.dma_start(h_all, h[bass.ds(b, 1), :, :].rearrange("a (t p) d -> p (a t) d", p=P))\
                  .then_inc(h_in, 16)
                def load_w(cols):
                    for j in range(3):
                        sp.dma_start(w_raw[:, :, j, :],
                                     wqkv[j, :, bass.ds(cols, P)].rearrange("(k p) n -> p k n", p=P))\
                          .then_inc(w_in, 16)

                def load_b(head, cols):
                    here = slice(head * DK, (head + 1) * DK)
                    for j in range(3):
                        sp.dma_start(b_qkv[:, j, here],
                                     bqkv[j, bass.ds(cols, DK)].partition_broadcast(P)).then_inc(b_in[head], 16)

                load_w(0)
                load_b(0, 0)
                load_b(1, DK)

                def pair(pr, last):
                    it = b * PAIRS + pr
                    split = sp.snap(it * 4 + 4)
                    biases_used = [sp.snap(it * ROWS + TT), sp.snap(it * ROWS + 2 * TT)]
                    divided = [sp.snap(it * COUPLES + COUPLES // 2), sp.snap(it * COUPLES + COUPLES)]
                    cols = [sp.snap(pr * P), sp.snap(pr * P + DK)]
                    next_cols = [sp.snap(pr * P + P), sp.snap(pr * P + (P + DK))]
                    all_stored = sp.snap(b * (16 * PAIRS) + (16 * PAIRS + 16))
                    all_projected = sp.snap(it * ROWS + ROWS)
                    if not last:
                        sp.wait_ge(w_lo, split)
                        load_w(next_cols[0])
                    for head in range(2):
                        if not last:
                            sp.wait_ge(biased, biases_used[head])
                            load_b(head, next_cols[head])
                        elif head == 1:
                            sp.wait_ge(qkv_done, all_projected)
                            for dst, src, k in ((wo_raw, wo, OC), (wg_raw, wgate_t, KC), (wu_raw, wup_t, KC),
                                                (wd_raw, wdown_t, MC)):
                                if dst is wd_raw:
                                    sp.wait_ge(o_stored[0], all_stored)
                                sp.dma_start(dst.rearrange("p (k n) -> p k n", k=k),
                                             src.rearrange("(k p) n -> p k n", p=P)).then_inc(cw_in, 16)
                        sp.wait_ge(normed, divided[head])
                        sp.dma_start(attn[bass.ds(b, 1), :, bass.ds(cols[head], DK)]
                                     .rearrange("a (t p) n -> p (a t) n", p=P),
                                     o_norm[:, :, head * DK:(head + 1) * DK]).then_inc(o_stored[head], 16)

                with sp.Fori(0, PAIRS - 1) as pr:
                    pair(pr, False)
                pair(PAIRS - 1, True)
                all_stored = sp.snap(b * (16 * PAIRS) + (16 * PAIRS + 16))
                sp.wait_ge(o_stored[1], all_stored)
                sp.dma_start(bo_sb[:, :], bo.partition_broadcast(P)).then_inc(bo_in, 16)
                def load_o(rows):
                    sp.dma_start(o_all, attn[bass.ds(b, 1), bass.ds(rows, TG * P), :]
                                 .rearrange("a (t p) n -> p (a t) n", p=P)).then_inc(o_in, 16)

                def load_h(rows):
                    sp.dma_start(h_g.rearrange("p (t d) -> p t d", t=TG),
                                 h[bass.ds(b, 1), bass.ds(rows, TG * P), :]
                                 .rearrange("a (t p) d -> p (a t) d", p=P)).then_inc(hg_in, 16)

                def store_out(rows):
                    sp.dma_start(out[bass.ds(b, 1), bass.ds(rows, TG * P), :]
                                 .rearrange("a (t p) d -> p (a t) d", p=P),
                                 out_g.rearrange("p (t d) -> p t d", t=TG)).then_inc(out_stored, 16)

                load_o(0)
                load_h(0)
                with sp.Fori(0, GROUPS - 1) as g:
                    c = b * GROUPS + g
                    turned_o, added, done = sp.snap(c * OC + OC), sp.snap(c + 1), sp.snap(c + 2)
                    rows, next_rows = sp.snap(g * (TG * P)), sp.snap(g * (TG * P) + TG * P)
                    sp.wait_ge(c_turned, turned_o)
                    load_o(next_rows)
                    sp.wait_ge(x_added, added)
                    load_h(next_rows)
                    sp.wait_ge(tile_done, done)
                    store_out(rows)
                last_done = sp.snap(b * GROUPS + GROUPS + 1)
                sp.wait_ge(tile_done, last_done)
                store_out((GROUPS - 1) * TG * P)
            sp.wait_ge(out_stored, 16 * BATCH * GROUPS + 16)
            for head in range(2):
                sp.wait_ge(o_stored[head], 16 * BATCH * PAIRS + 16)

        @block.gpsimd
        def _(pool):
            pool.wait_ge(const_in, 16 * 8)
            def tile(n, head, t):
                x = qkv_f[t % 4]
                here = slice(head * DK, (head + 1) * DK)
                pool.wait_ge(qkv_copied, n + 1)
                nc.gpsimd.tensor_tensor(x[:, :, :], x[:, :, :], b_qkv[:, :, here], ALU.add).then_inc(biased, 1)
                pool.wait_ge(biased, n + 1)
                pool.wait_ge(roped, 2 * n + 8)
                x4 = x[:, 0:2, :].rearrange("p v (a d) -> p (v a) d", a=2)
                nc.gpsimd.tensor_tensor(rope_s[:, :, :].rearrange("p v (a d) -> p (v a) d", a=2), x4,
                                        sin_sb[:, t, :].unsqueeze(1).broadcast_to([P, 4, DK // 2]),
                                        ALU.mult).then_inc(rope_mul, 1)
                pool.wait_ge(rope_mul, 2 * n + 1)
                nc.gpsimd.tensor_tensor(x4, x4, cos_sb[:, t, :].unsqueeze(1).broadcast_to([P, 4, DK // 2]),
                                        ALU.mult).then_inc(rope_mul, 1)
                pool.wait_ge(rope_mul, 2 * n + 2)
                pool.wait_ge(qk_turned, n + 1)
                half = DK // 2
                for a, op in ((0, ALU.subtract), (1, ALU.add)):
                    c = x[:, 0:2, a * half:(a + 1) * half].unsqueeze(2).broadcast_to([P, 2, 2, half])
                    s = rope_s[:, :, (1 - a) * half:(2 - a) * half].unsqueeze(2).broadcast_to([P, 2, 2, half])
                    nc.gpsimd.tensor_tensor(rope_d[t % 2][:, :, :, a * half:(a + 1) * half], c, s, op)\
                      .then_inc(roped, 1)
                pool.wait_ge(v_hi, n + 1)
                nc.gpsimd.tensor_tensor(v_st[:, t, head, 1, :], x[:, 2, :], v_st[:, t, head, 0, :].bitcast(F32),
                                        ALU.subtract).then_inc(v_lo, 1)

            with pool.Fori(0, BATCH * PAIRS) as it:
                for j in range(ROWS):
                    head, t = row(j)
                    if t == 0:
                        pool.wait_ge(b_scaled, it * 2 + (head + 1))
                    tile(it * ROWS + j, head, t)

        @block.scalar
        def _(act):
            act.wait_ge(const_in, 16 * 8)
            act.wait_ge(primed, 1)
            with act.Fori(0, BATCH) as b:
                act.wait_ge(out_stored, b * (16 * GROUPS) + 16)
                act.wait_ge(a_eps, b + 1)
                nc.scalar.activation(std[:, :], mv[:, :, 1], ACT.Sqrt).then_inc(a_std, 1)
                for i in range(KC * GROUPS):
                    k, g = i // GROUPS, i % GROUPS
                    act.wait_ge(a_turned, b * 8 + (i + 1))
                    if i >= 2:
                        act.wait_ge(a_lo, b * 8 + (i - 1))
                    nc.scalar.activation(hn_f[i % 2], s_bank[i % 4], ACT.Identity,
                                         bias=bet[:, k:k + 1], scale=gam[:, k:k + 1]).then_inc(a_affine, 1)
                    act.wait_ge(a_affine, b * 8 + (i + 1))
                    nc.scalar.activation(hn[:, 0, k, 512 * g:512 * (g + 1)], hn_f[i % 2], ACT.Copy)\
                      .then_inc(a_hi, 1)

                def weights(n, head):
                    act.wait_ge(w_in, n * 48 + 48)
                    wh = w_hl[:, 0, :, :].rearrange("p k (j n) -> p k j n", j=3)
                    here = slice(head * DK, (head + 1) * DK)
                    nc.scalar.activation(wh[:, :, 0, here], w_raw[:, :, 0, here], ACT.Copy, scale=SCALE)\
                      .then_inc(w_hi, 1)
                    nc.scalar.activation(wh[:, :, 1:3, here], w_raw[:, :, 1:3, here], ACT.Copy).then_inc(w_hi, 1)

                def bias(n, head):
                    act.wait_ge(b_in[head], n * 48 + 48)
                    here = slice(head * DK, (head + 1) * DK)
                    nc.scalar.activation(b_qkv[:, 0, here], b_qkv[:, 0, here], ACT.Copy, scale=SCALE)\
                      .then_inc(b_scaled, 1)

                def run(seq, it):
                    def copy_qkv(j):
                        n = it * ROWS + j
                        act.wait_ge(qkv_done, n + 1)
                        act.wait_ge(v_lo, n + 1)
                        act.wait_ge(roped, n * 2 + 2)
                        nc.scalar.activation(qkv_f[j % 4][:, :, :], bank("mul", j)[:, 0:3 * DK]
                                             .rearrange("p (j d) -> p j d", j=3), ACT.Copy).then_inc(qkv_copied, 1)

                    def copy_v(j):
                        head, t = row(j)
                        act.wait_ge(biased, it * ROWS + (j + 1))
                        nc.scalar.activation(v_st[:, t, head, 0, :], qkv_f[j % 4][:, 2, :], ACT.Copy).then_inc(v_hi, 1)

                    def qk_hi_part(j):
                        head, t = row(j)
                        act.wait_ge(qk_turned, it * ROWS + (j + 3))
                        nc.scalar.activation(qk_hi[:, head:4:2, t * P:(t + 1) * P],
                                             bank("qk", j)[:, 0:2 * P].rearrange("p (v n) -> p v n", v=2), ACT.Copy)\
                          .then_inc(qk_hi_done, 1)

                    def hi_part(x):
                        j, u = x
                        n, t = width(x), row(j)[1]
                        if j - 4 in seq.rows:
                            act.wait_ge(pv_done, it * COUPLES + (j // 2 - 1))
                        act.wait_ge(turned, it * NU + (unit_no(x) + 1))
                        nc.scalar.activation(
                            pt_hi[:, (j // 2) % 2, 4 * u:4 * u + n, (t % 2) * P:(t % 2 + 1) * P],
                            bank("turn", j, u)[:, 0:n * P].rearrange("p (k q) -> p k q", k=n), ACT.Copy)\
                          .then_inc(p_hi, 1)

                    def exp_part(x):
                        j, u = x
                        head, t = row(j)
                        w = width(x) * P
                        act.wait_ge(maxed, it * ROWS + (j + 1))
                        if j - 2 in seq.rows and u == 0:
                            act.wait_ge(turned, it * NU + units_to(j - 2))
                        nc.scalar.activation(probs[:, j % 2, 512 * u:512 * u + w],
                                             s_bank[unit_no(x) % 4][:, 0:w], ACT.Exp,
                                             bias=nmax[:, j % 2:j % 2 + 1],
                                             accum_out=rsum[:, head * TT + t, u:u + 1]).then_inc(exped, 1)

                    def copy_out(c):
                        act.wait_ge(pv_done, it * COUPLES + (c + 1))
                        if 2 * c - 2 in seq.rows:
                            act.wait_ge(o_turned, it * COUPLES + c)
                        nc.scalar.activation(o_sum[:, :], o_ps[:, 0:2 * P], ACT.Copy).then_inc(o_out, 1)

                    for i in seq.steps:
                        tr, ex = seq.units(i, TURN), seq.units(i, EXP)
                        for k in range(4):
                            for x in tr[k:k + 1]:
                                hi_part(x)
                            for x in ex[k:k + 1]:
                                exp_part(x)
                            if k == 0:
                                for j in seq.tile(i, MUL - 1):
                                    copy_v(j)
                                for j in seq.tile(i, MUL):
                                    copy_qkv(j)
                            if k == 1:
                                for j in seq.tile(i, TURN_QK):
                                    qk_hi_part(j)
                        if i % 2 == 1:
                            for c in seq.couple(i, PV):
                                copy_out(c)
                        if i == BIAS_B:
                            bias(it, 1)
                        if seq is not LAST:
                            if i == WEIGHTS_A:
                                act.wait_ge(qkv_done, it * ROWS + TT)
                                weights(it + 1, 0)
                            if i == WEIGHTS_B:
                                act.wait_ge(qkv_done, it * ROWS + 2 * TT)
                                weights(it + 1, 1)
                            if i == BIAS_A:
                                bias(it + 1, 0)

                for head in range(2):
                    weights(b * PAIRS, head)
                bias(b * PAIRS, 0)
                run(FIRST, b * PAIRS)
                with act.Fori(1, PAIRS - 1) as pr:
                    run(MIDDLE, b * PAIRS + pr)
                run(LAST, b * PAIRS + (PAIRS - 1))

                act.wait_ge(cw_in, b * 64 + 64)
                for dst, raw in ((wo_hl, wo_raw), (wg_hl, wg_raw), (wu_hl, wu_raw), (wd_hl, wd_raw)):
                    nc.scalar.activation(dst[0], raw, ACT.Copy).then_inc(cw_hi, 1)

                def attn_hi(c):
                    for k in range(OC):
                        act.wait_ge(c_turned, c * OC + (k + 1))
                        nc.scalar.activation(o_t[0][:, 512 * k:512 * (k + 1)], gu_bank[k % 4], ACT.Copy)\
                          .then_inc(c_hi, 1)

                def root(n):
                    act.wait_ge(ln_eps, n + 1)
                    nc.scalar.activation(std[:, 0:TG], mv[:, 0:TG, 1], ACT.Sqrt).then_inc(ln_std, 1)

                def ffn_hi(c):
                    act.wait_ge(ln_rows, c * TG + TG)
                    nc.scalar.activation(x1_keep, x1_g, ACT.Copy).then_inc(x_kept, 1)
                    for k in range(KC):
                        act.wait_ge(x_turned, c * KC + (k + 1))
                        nc.scalar.activation(x1_t[0][:, 512 * k:512 * (k + 1)], gu_bank[k], ACT.Copy)\
                          .then_inc(x_hi, 1)
                    for m in range(MC + 1):
                        if m < MC:
                            act.wait_ge(gate_up, c * MC + (m + 1))
                            if m >= 2:
                                act.wait_ge(hid_done, c * MC + (m - 1))
                            nc.scalar.activation(silu_g[m % 2], gu_bank[2 - 2 * (m % 2)], ACT.Silu, scale=DEQ)\
                              .then_inc(silu_done, 1)
                        if m >= 1:
                            act.wait_ge(hid_done, c * MC + m)
                            nc.scalar.activation(hid_t[0][:, 512 * (m - 1):512 * m], hid_f[(m - 1) % 2], ACT.Copy)\
                              .then_inc(hid_hi, 1)

                attn_hi(b * GROUPS)
                root(b * (2 * GROUPS))
                with act.Fori(0, GROUPS - 1) as g:
                    c = b * GROUPS + g
                    attn_hi(c + 1)
                    ffn_hi(c)
                    root(c * 2 + 1)
                    root(c * 2 + 2)
                ffn_hi(b * GROUPS + (GROUPS - 1))
                root(b * (2 * GROUPS) + (2 * GROUPS - 1))

        @block.vector
        def _(dve):
            nc.vector.memset(rsum[:, :, :], 0.0).then_inc(ones_ready, 1)
            nc.vector.memset(rstd[:, 0:1], 0.0).then_inc(qk_turned, 2)
            nc.vector.memset(rstd[:, 1:2], 0.0).then_inc(v_lo, 4)
            nc.vector.memset(rstd[:, 2:3], 0.0).then_inc(roped, 8)
            nc.vector.memset(nmax[:, 1:2], 0.0).then_inc(tile_done, 1)
            nc.vector.memset(rinv[:, :], 0.0).then_inc(out_stored, 16)
            nc.vector.memset(rtot[:, 0:8], 0.0).then_inc(o_stored[0], 16)
            nc.vector.memset(rtot[:, 8:16], 0.0).then_inc(o_stored[1], 16)
            nc.vector.memset(pause[:, :], 0.0).then_inc(z_added, 1)
            nc.vector.memset(rtot[:, 16:32], 0.0).then_inc(primed, 1)
            with dve.Fori(0, BATCH) as b:
                dve.wait_ge(h_in, b * 16 + 16)
                for t in range(TT):
                    nc.vector.bn_stats(stats[:, t, :], h_all[:, t, :]).then_inc(a_stats, 1)
                dve.wait_ge(a_stats, b * TT + TT)
                nc.vector.memset(pause[:, :], 0.0).then_inc(a_aggr, 1)
                for t in range(TT):
                    nc.vector.bn_aggr(mv[:, t, :], stats[:, t, :]).then_inc(a_aggr, 1)
                dve.wait_ge(a_aggr, b * (TT + 1) + (TT + 1))
                nc.vector.tensor_scalar(mv[:, :, 1], mv[:, :, 1], EPS, None, ALU.add).then_inc(a_eps, 1)
                dve.wait_ge(a_std, b + 1)
                nc.vector.reciprocal(rstd[:, :], std[:, :]).then_inc(a_rstd, 1)
                dve.wait_ge(a_rstd, b + 1)
                for t in range(TT):
                    nc.vector.tensor_scalar(h_all[:, t, :], h_all[:, t, :], mv[:, t, 0:1], rstd[:, t:t + 1],
                                            ALU.subtract, ALU.mult).then_inc(a_norm, 1)
                for i in range(KC * GROUPS):
                    k, g = i // GROUPS, i % GROUPS
                    dve.wait_ge(a_hi, b * 8 + (i + 1))
                    nc.vector.tensor_tensor(hn[:, 1, k, 512 * g:512 * (g + 1)], hn_f[i % 2],
                                            hn[:, 0, k, 512 * g:512 * (g + 1)].bitcast(F32), ALU.subtract)\
                      .then_inc(a_lo, 1)

                def weights(n, head):
                    dve.wait_ge(w_in, n * 48 + 48)
                    dve.wait_ge(w_hi, n * 4 + (2 * head + 2))
                    wv = w_hl[:, :, :, :].rearrange("p a k (j n) -> p a k j n", j=3)
                    here = slice(head * DK, (head + 1) * DK)
                    nc.vector.scalar_tensor_tensor(
                        wv[:, 1, :, 0, here], w_raw[:, :, 0, here], SCALE, wv[:, 0, :, 0, here].bitcast(F32),
                        ALU.mult, ALU.subtract).then_inc(w_lo, 1)
                    nc.vector.tensor_tensor(
                        wv[:, 1, :, 1:3, here], w_raw[:, :, 1:3, here], wv[:, 0, :, 1:3, here].bitcast(F32),
                        ALU.subtract).then_inc(w_lo, 1)

                def run(seq, it):
                    def qk_lo_part(j):
                        head, t = row(j)
                        here = slice(t * P, (t + 1) * P)
                        src = bank("qk", j)
                        dve.wait_ge(qk_hi_done, it * ROWS + (j + 1))
                        nc.vector.tensor_tensor(k_lo[:, head, here], src[:, P:2 * P],
                                                qk_hi[:, 2 + head, here].bitcast(F32), ALU.subtract)\
                          .then_inc(qk_lo_done, 1)
                        nc.vector.tensor_tensor(qk_hi[DK:P, head, here], src[DK:P, 0:P],
                                                qk_hi[DK:P, head, here].bitcast(F32), ALU.subtract)\
                          .then_inc(qk_lo_done, 1)

                    def unit_max(x):
                        j, u = x
                        n = len(row_units(j))
                        if j - 2 in seq.rows and u == 0:
                            dve.wait_ge(exped, it * NU + units_to(j - 2))
                        dve.wait_ge(scored, it * NU + (unit_no(x) + 1))
                        scores = s_bank[unit_no(x) % 4][:, 0:width(x) * P]
                        if n == 1:
                            nc.vector.tensor_reduce(nmax[:, j % 2:j % 2 + 1], scores, AX.X, ALU.max, negate=True)\
                              .then_inc(maxed, 1)
                            return
                        nc.vector.tensor_reduce(nmax_part[:, j % 2, u:u + 1], scores, AX.X, ALU.max, negate=True)\
                          .then_inc(max_part, 1)
                        if u == n - 1:
                            dve.wait_ge(max_part, it * NPART + parts_to(j))
                            nc.vector.tensor_reduce(nmax[:, j % 2:j % 2 + 1], nmax_part[:, j % 2, 0:n],
                                                    AX.X, ALU.min).then_inc(maxed, 1)

                    def lo_part(x):
                        j, u = x
                        n, t = width(x), row(j)[1]
                        dve.wait_ge(p_hi, it * NU + (unit_no(x) + 1))
                        here = (slice(None), (j // 2) % 2, slice(4 * u, 4 * u + n),
                                slice((t % 2) * P, (t % 2 + 1) * P))
                        nc.vector.tensor_tensor(
                            pt_lo[here], bank("turn", j, u)[:, 0:n * P].rearrange("p (k q) -> p k q", k=n),
                            pt_hi[here].bitcast(F32), ALU.subtract).then_inc(p_lo, 1)

                    def invert(c):
                        head, t = row(2 * c)
                        rows = slice(head * TT + t, head * TT + t + 2)
                        nc.vector.tensor_reduce(rtot[:, rows], rsum[:, rows, :], AX.X, ALU.add).then_inc(r_sum, 1)
                        dve.wait_ge(r_sum, it * COUPLES + (c + 1))
                        nc.vector.reciprocal(rinv[:, rows], rtot[:, rows]).then_inc(r_inv, 1)

                    def divide(c):
                        head, t = row(2 * c)
                        rows = slice(head * TT + t, head * TT + t + 2)
                        if t == 0:
                            dve.wait_ge(o_stored[head], it * 16 + 16)
                        dve.wait_ge(o_turned, it * COUPLES + (c + 1))
                        dve.wait_ge(r_inv, it * COUPLES + (c + 1))
                        nc.vector.tensor_tensor(
                            o_norm[:, t:t + 2, head * DK:(head + 1) * DK],
                            bank("out", 2 * c)[:, 0:2 * DK].rearrange("p (a d) -> p a d", a=2),
                            rinv[:, rows].unsqueeze(2).broadcast_to([P, 2, DK]), ALU.mult).then_inc(normed, 1)

                    for i in seq.steps:
                        tr, sc = seq.units(i, TURN), seq.units(i, 0)
                        for k in range(4):
                            for x in tr[k:k + 1]:
                                lo_part(x)
                            for x in sc[k:k + 1]:
                                unit_max(x)
                            if k == 0:
                                for c in seq.final(i):
                                    divide(c)
                            if k == 1:
                                for j in seq.tile(i, TURN_QK):
                                    qk_lo_part(j)
                        if i % 2 == 0:
                            for c in seq.couple(i, PV):
                                invert(c)
                        if seq is not LAST:
                            if i == WEIGHTS_A:
                                weights(it + 1, 0)
                            if i == WEIGHTS_B:
                                weights(it + 1, 1)

                for head in range(2):
                    weights(b * PAIRS, head)
                run(FIRST, b * PAIRS)
                with dve.Fori(1, PAIRS - 1) as pr:
                    run(MIDDLE, b * PAIRS + pr)
                run(LAST, b * PAIRS + (PAIRS - 1))

                for n, (dst, raw) in enumerate(((wo_hl, wo_raw), (wg_hl, wg_raw), (wu_hl, wu_raw),
                                                (wd_hl, wd_raw))):
                    dve.wait_ge(cw_hi, b * 4 + (n + 1))
                    nc.vector.tensor_tensor(dst[1], raw, dst[0].bitcast(F32), ALU.subtract).then_inc(cw_lo, 1)

                def attn_lo(c):
                    for k in range(OC):
                        dve.wait_ge(c_hi, c * OC + (k + 1))
                        nc.vector.tensor_tensor(o_t[1][:, 512 * k:512 * (k + 1)], gu_bank[k % 4],
                                                o_t[0][:, 512 * k:512 * (k + 1)].bitcast(F32), ALU.subtract)\
                          .then_inc(c_lo, 1)

                def norm(x, n, rows_done):
                    for t in range(TG):
                        nc.vector.bn_stats(stats[:, t, :], x[:, t * DM:(t + 1) * DM]).then_inc(ln_stats, 1)
                    dve.wait_ge(ln_stats, n * (2 * TG + 1) + TG)
                    nc.vector.memset(pause[:, :], 0.0).then_inc(ln_stats, 1)
                    for t in range(TG):
                        nc.vector.bn_aggr(mv[:, t, :], stats[:, t, :]).then_inc(ln_stats, 1)
                    dve.wait_ge(ln_stats, n * (2 * TG + 1) + (2 * TG + 1))
                    nc.vector.tensor_scalar(mv[:, 0:TG, 1], mv[:, 0:TG, 1], EPS, None, ALU.add).then_inc(ln_eps, 1)
                    dve.wait_ge(ln_std, n + 1)
                    nc.vector.reciprocal(rstd[:, 0:TG], std[:, 0:TG]).then_inc(ln_rstd, 1)
                    dve.wait_ge(ln_rstd, n + 1)
                    for t in range(TG):
                        nc.vector.tensor_scalar(x[:, t * DM:(t + 1) * DM], x[:, t * DM:(t + 1) * DM],
                                                mv[:, t, 0:1], rstd[:, t:t + 1],
                                                ALU.subtract, ALU.mult).then_inc(rows_done, 1)

                def first_norm(c, n, first):
                    dve.wait_ge(hg_in, c * 16 + 16)
                    dve.wait_ge(y_done, c + 1)
                    if not first:
                        dve.wait_ge(x_kept, c)
                        dve.wait_ge(x_turned, c * KC)
                    nc.vector.scalar_tensor_tensor(x1_g, h_g, 2.0, y_ps, ALU.mult, ALU.add).then_inc(x_added, 1)
                    dve.wait_ge(x_added, c + 1)
                    if first:
                        dve.wait_ge(bo_in, c * 4 + 16)
                    x3 = x1_g.rearrange("p (t d) -> p t d", t=TG)
                    nc.vector.tensor_tensor(x3, x3, bo_sb[:, :].unsqueeze(1).broadcast_to([P, TG, DM]),
                                            ALU.add).then_inc(x_biased, 1)
                    dve.wait_ge(x_biased, c + 1)
                    norm(x1_g, n, ln_rows)

                def ffn_lo(c):
                    for k in range(KC):
                        dve.wait_ge(x_hi, c * KC + (k + 1))
                        nc.vector.tensor_tensor(x1_t[1][:, 512 * k:512 * (k + 1)], gu_bank[k],
                                                x1_t[0][:, 512 * k:512 * (k + 1)].bitcast(F32), ALU.subtract)\
                          .then_inc(x_lo, 1)
                    for m in range(MC + 1):
                        if m < MC:
                            dve.wait_ge(silu_done, c * MC + (m + 1))
                            if m >= 2:
                                dve.wait_ge(hid_hi, c * MC + (m - 1))
                                dve.wait_ge(hid_lo, c * MC + (m - 1))
                            nc.vector.scalar_tensor_tensor(hid_f[m % 2], gu_bank[3 - 2 * (m % 2)], DEQ,
                                                           silu_g[m % 2], ALU.mult, ALU.mult).then_inc(hid_done, 1)
                        if m >= 1:
                            dve.wait_ge(hid_hi, c * MC + m)
                            nc.vector.tensor_tensor(hid_t[1][:, 512 * (m - 1):512 * m], hid_f[(m - 1) % 2],
                                                    hid_t[0][:, 512 * (m - 1):512 * m].bitcast(F32), ALU.subtract)\
                              .then_inc(hid_lo, 1)

                def second_norm(c, n):
                    dve.wait_ge(z_done, c + 1)
                    dve.wait_ge(x_kept, c + 1)
                    dve.wait_ge(out_stored, c * 16 + 16)
                    nc.vector.scalar_tensor_tensor(out_g, z_ps, DEQ, x1_keep, ALU.mult, ALU.add)\
                      .then_inc(z_added, 1)
                    dve.wait_ge(z_added, c + 2)
                    norm(out_g, n, out_rows)
                    dve.wait_ge(out_rows, c * TG + TG)
                    nc.vector.memset(pause[:, :], 0.0).then_inc(tile_done, 1)

                attn_lo(b * GROUPS)
                first_norm(b * GROUPS, b * (2 * GROUPS), True)
                with dve.Fori(0, GROUPS - 1) as g:
                    c = b * GROUPS + g
                    attn_lo(c + 1)
                    ffn_lo(c)
                    first_norm(c + 1, c * 2 + 1, False)
                    second_norm(c, c * 2 + 2)
                ffn_lo(b * GROUPS + (GROUPS - 1))
                second_norm(b * GROUPS + (GROUPS - 1), b * (2 * GROUPS) + (2 * GROUPS - 1))

        @block.tensor
        def _(pe):
            def product(dst, lhs, rhs, first=True, last=True):
                nc.tensor.matmul(dst, lhs[0], rhs[0], start=first, stop=False)
                nc.tensor.matmul(dst, lhs[1], rhs[0], start=False, stop=False)
                return nc.tensor.matmul(dst, lhs[0], rhs[1], start=False, stop=last)

            pe.wait_ge(const_in, 16 * 8)
            pe.wait_ge(ones_ready, 1)
            pe.wait_ge(primed, 1)
            with pe.Fori(0, BATCH) as b:
                for i in range(KC * GROUPS):
                    k, g = i // GROUPS, i % GROUPS
                    if k == 0:
                        pe.wait_ge(a_norm, b * TT + 4 * (g + 1))
                    if i >= 4:
                        pe.wait_ge(a_affine, b * 8 + (i - 3))
                    for j in range(4):
                        last = nc.tensor.transpose(s_bank[i % 4][:, j * P:(j + 1) * P],
                                                   h_all[:, 4 * g + j, k * P:(k + 1) * P], id_f[:, :])
                    last.then_inc(a_turned, 1)

                def run(seq, it):
                    def ring_free(kind, j, u=0):
                        y = use_before(seq, (kind, j, u))
                        if y is None:
                            return
                        kind, j, u = y
                        if kind == "turn":
                            pe.wait_ge(p_lo, it * NU + (unit_no((j, u)) + 1))
                        elif kind == "out":
                            pe.wait_ge(normed, it * COUPLES + (j // 2 + 1))
                        elif kind == "mul":
                            pe.wait_ge(qkv_copied, it * ROWS + (j + 1))
                        else:
                            pe.wait_ge(qk_lo_done, it * (2 * ROWS) + (2 * j + 2))

                    def multiply(j):
                        head, t = row(j)
                        ring_free("mul", j)
                        if t == 0:
                            pe.wait_ge(w_lo, it * 4 + (4 * (j // ROWS) + 2 * head + 2))
                        here = slice(t * P, (t + 1) * P)
                        for k in range(KC):
                            last = product(bank("mul", j)[:, 0:3 * DK], [hn[:, a, k, here] for a in range(2)],
                                           [w_hl[:, a, k, :].rearrange("p (j h d) -> p j h d", j=3, h=2)[:, :, head, :]
                                            for a in range(2)], first=(k == 0), last=(k == KC - 1))
                        last.then_inc(qkv_done, 1)

                    def turn_qk(j):
                        ring_free("qk", j)
                        pe.wait_ge(roped, it * (2 * ROWS) + (2 * j + 10))
                        for v in range(2):
                            last = nc.tensor.transpose(bank("qk", j)[:, v * P:(v + 1) * P],
                                                       rope_d[j % 2][:, v, :, :].rearrange("p a d -> p (a d)"),
                                                       id_f[:, :])
                        last.then_inc(qk_turned, 1)

                    def scores(x):
                        j, u = x
                        head, t = row(j)
                        q = qk_hi[:, head, t * P:(t + 1) * P]
                        n = unit_no(x)
                        k0, w = 512 * u, width(x) * P
                        dst = s_bank[n % 4][:, 0:w]
                        diag = x == row_units(j)[-1]
                        if u == 0:
                            pe.wait_ge(qk_lo_done, it * (2 * ROWS) + (2 * j + 2))
                        if n >= 4 or seq is not FIRST:
                            pe.wait_ge(exped, it * NU + (n - 3))
                        nc.tensor.matmul(dst, q, qk_hi[:, 2 + head, k0:k0 + w], start=True, stop=False)
                        last = nc.tensor.matmul(dst, q, k_lo[:, head, k0:k0 + w], start=False, stop=not diag)
                        if diag:
                            last = nc.tensor.matmul(dst[:, w - P:w], id_b[:, :], mask_b[:, :],
                                                    start=False, stop=True)
                        last.then_inc(scored, 1)

                    def turn_probs(x):
                        j, u = x
                        ring_free("turn", j, u)
                        pe.wait_ge(exped, it * NU + (unit_no(x) + 1))
                        for k in range(width(x)):
                            last = nc.tensor.transpose(bank("turn", j, u)[:, k * P:(k + 1) * P],
                                                       probs[:, j % 2, (4 * u + k) * P:(4 * u + k + 1) * P],
                                                       id_f[:, :])
                        last.then_inc(turned, 1)

                    def pv_part(c, half, part):
                        head, t0 = row(2 * c)
                        n = t0 + 2
                        e = 4 * half + part
                        if e == 0:
                            pe.wait_ge(p_lo, it * NU + units_to(2 * c + 1))
                            pe.wait_ge(v_lo, it * ROWS + (2 * c + 6))
                            if 2 * c - 2 in seq.rows:
                                pe.wait_ge(o_out, it * COUPLES + c)
                        for k in range(e * n // 8, (e + 1) * n // 8):
                            c0 = P if k == n - 1 else 0
                            v = v_st[:, k, head, :, :].rearrange("p a d -> p (a d)")
                            for src in (pt_hi, pt_lo):
                                last = nc.tensor.matmul(o_ps[:, c0:2 * P], v, src[:, c % 2, k, c0:2 * P],
                                                        start=(k == 0 and src is pt_hi),
                                                        stop=(k == n - 1 and src is pt_lo),
                                                        skip_group_check=True)
                        if e == 7:
                            last.then_inc(pv_done, 1)

                    def turn_out(c):
                        ring_free("out", 2 * c)
                        pe.wait_ge(o_out, it * COUPLES + (c + 1))
                        for a in range(2):
                            last = nc.tensor.matmul(bank("out", 2 * c)[:, a * DK:(a + 1) * DK],
                                                    o_sum[:, a * P:(a + 1) * P], id_2[:, :],
                                                    start=True, stop=True)
                        last.then_inc(o_turned, 1)

                    if seq is FIRST:
                        pe.wait_ge(a_lo, b * 8 + 8)
                    for i in seq.steps:
                        tr, sc = seq.units(i, TURN), seq.units(i, 0)
                        for k in range(4):
                            for x in tr[k:k + 1]:
                                turn_probs(x)
                            if k == 0:
                                for c in seq.final(i):
                                    turn_out(c)
                            for c in seq.couple(i, PV):
                                pv_part(c, i % 2, k)
                            if k == 0:
                                for j in seq.tile(i, MUL):
                                    multiply(j)
                            if k == 1:
                                for j in seq.tile(i, TURN_QK):
                                    turn_qk(j)
                            for x in sc[k:k + 1]:
                                scores(x)

                run(FIRST, b * PAIRS)
                with pe.Fori(1, PAIRS - 1) as pr:
                    run(MIDDLE, b * PAIRS + pr)
                run(LAST, b * PAIRS + (PAIRS - 1))

                def project_out(c):
                    for t in range(TG):
                        for k in range(OC):
                            last = product(y_ps[:, t * DM:(t + 1) * DM],
                                           [x[:, 512 * k + t * P:512 * k + (t + 1) * P] for x in o_t],
                                           [x[:, k * DM:(k + 1) * DM] for x in wo_hl],
                                           first=(k == 0), last=(k == OC - 1))
                    last.then_inc(y_done, 1)

                def turn_attn(c):
                    pe.wait_ge(o_in, c * 16 + 16)
                    for k in range(OC):
                        if k >= 4:
                            pe.wait_ge(c_lo, c * OC + (k - 3))
                        for t in range(TG):
                            last = nc.tensor.transpose(gu_bank[k % 4][:, t * P:(t + 1) * P],
                                                       o_all[:, t, k * P:(k + 1) * P], id_f[:, :])
                        last.then_inc(c_turned, 1)

                def ffn_up(c, also_next):
                    pe.wait_ge(ln_rows, c * TG + TG)
                    if also_next:
                        pe.wait_ge(c_lo, c * OC + 2 * OC)
                    for k in range(KC):
                        for t in range(TG):
                            last = nc.tensor.transpose(gu_bank[k][:, t * P:(t + 1) * P],
                                                       x1_g[:, t * DM + k * P:t * DM + (k + 1) * P], id_f[:, :])
                        last.then_inc(x_turned, 1)
                    pe.wait_ge(x_lo, c * KC + KC)
                    for m in range(MC):
                        if m >= 2:
                            pe.wait_ge(hid_done, c * MC + (m - 1))
                        for dst, w in ((gu_bank[2 - 2 * (m % 2)], wg_hl), (gu_bank[3 - 2 * (m % 2)], wu_hl)):
                            for k in range(KC):
                                last = product(dst, [x[:, k * HID + m * P:k * HID + (m + 1) * P] for x in w],
                                               [x[:, 512 * k:512 * (k + 1)] for x in x1_t],
                                               first=(k == 0), last=(k == KC - 1))
                        last.then_inc(gate_up, 1)

                def ffn_down(c):
                    pe.wait_ge(hid_lo, c * MC + MC)
                    pe.wait_ge(z_added, c + 1)
                    for t in range(TG):
                        for m in range(MC):
                            last = product(z_ps[:, t * DM:(t + 1) * DM],
                                           [x[:, 512 * m + t * P:512 * m + (t + 1) * P] for x in hid_t],
                                           [x[:, m * DM:(m + 1) * DM] for x in wd_hl],
                                           first=(m == 0), last=(m == MC - 1))
                    last.then_inc(z_done, 1)

                turn_attn(b * GROUPS)
                pe.wait_ge(cw_lo, b * 4 + 4)
                pe.wait_ge(c_lo, b * (GROUPS * OC) + OC)
                project_out(b * GROUPS)
                with pe.Fori(0, GROUPS - 1) as g:
                    c = b * GROUPS + g
                    turn_attn(c + 1)
                    ffn_up(c, True)
                    project_out(c + 1)
                    ffn_down(c)
                ffn_up(b * GROUPS + (GROUPS - 1), False)
                ffn_down(b * GROUPS + (GROUPS - 1))


_INS = ["h", "gamma", "beta", "wqkv", "bqkv", "wo", "bo", "wgate_t", "wup_t", "wdown_t",
        "cos", "sin", "ident", "ident2", "mask"]


def kernel(L0_attn_h, L0_attn_gamma, L0_attn_beta, L0_attn_Wq, L0_attn_bq, L0_attn_Wk, L0_attn_bk,
           L0_attn_Wv, L0_attn_bv, L0_attn_Wo, L0_attn_bo, L0_ffn_w_gate, L0_ffn_w_up, L0_ffn_w_down):
    import ml_dtypes
    import numpy as np
    import concourse.bacc as bacc
    from concourse.bass_utils import run_bass_kernel_spmd

    theta = np.float32(1.0) / np.float32(10000.0) ** (np.arange(0, DK, 2, dtype=np.float32) / np.float32(DK))
    angle = np.arange(SEQ, dtype=np.float32)[:, None] * theta[None, :].astype(np.float32)
    tiled = angle.reshape(TT, P, DK // 2).transpose(1, 0, 2)
    eye = np.eye(P, dtype=np.float32)
    later = np.triu(np.full((P, P), MASKED, np.float32), 1)

    arrays = {
        "h": L0_attn_h, "gamma": np.reshape(L0_attn_gamma, (KC, P)).T, "beta": np.reshape(L0_attn_beta, (KC, P)).T,
        "wqkv": np.stack([L0_attn_Wq, L0_attn_Wk, L0_attn_Wv]),
        "bqkv": np.stack([L0_attn_bq, L0_attn_bk, L0_attn_bv]),
        "wo": L0_attn_Wo, "bo": L0_attn_bo,
        "wgate_t": np.transpose(L0_ffn_w_gate), "wup_t": np.transpose(L0_ffn_w_up),
        "wdown_t": np.transpose(L0_ffn_w_down),
        "cos": np.cos(tiled).astype(np.float32), "sin": np.sin(tiled).astype(np.float32),
        "ident": eye, "ident2": np.concatenate([eye[:DK, :DK]] * 2),
        "mask": np.stack([eye, later]).astype(ml_dtypes.bfloat16),
    }
    arrays = {n: np.ascontiguousarray(a) for n, a in arrays.items()}
    nc = bacc.Bacc("TRN2", target_bir_lowering=False, num_devices=1)
    args = [nc.dram_tensor(f"in_{n}", arrays[n].shape, mybir.dt.from_np(arrays[n].dtype),
                           kind="ExternalInput").ap() for n in _INS]
    attn = nc.dram_tensor("attn", (BATCH, SEQ, HEADS * DK), F32, kind="Internal").ap()
    out = nc.dram_tensor("out", (BATCH, SEQ, DM), F32, kind="ExternalOutput").ap()
    postln_block_kernel(nc, *args, attn, out)
    r = run_bass_kernel_spmd(nc, [{f"in_{n}": arrays[n] for n in _INS}], core_ids=[0])
    return r.results[0]["out"]
```

```python
from contextlib import ExitStack

import concourse.bass as bass
from concourse import mybir

ALU = mybir.AluOpType
ACT = mybir.ActivationFunctionType
AX = mybir.AxisListType
F32 = mybir.dt.float32
F32R = mybir.dt.float32r
BF16 = mybir.dt.bfloat16
I32 = mybir.dt.int32

P = 128
BATCH, SEQ, DM = 2, 2048, 256
HEADS, DK = 16, 64
HID = 768
PAIRS = HEADS // 2
TT = SEQ // P
KC = DM // P
MC = HID // P
QKV = 3 * P
TG = 4
GROUPS = TT // TG
OC = HEADS * DK // P
SCALE = DK ** -0.5
DEQ = 1.0 / 127.0
EPS = 1e-5
MASKED = -1e30
ROWS = 2 * TT
COUPLES = ROWS // 2


def postln_block_kernel(nc, h, gamma, beta, wqkv, bqkv, wo, bo, wgate_t, wup_t, wdown_t,
                        cos, sin, ident, ident2, mask, attn, out):
    with ExitStack() as ctx:
        def sb(name, shape, dt):
            return ctx.enter_context(nc.sbuf_tensor(name, shape, dt))

        def sem(name):
            return ctx.enter_context(nc.semaphore(name))

        cos_sb = sb("cos_sb", [P, TT, DK // 2], F32)
        sin_sb = sb("sin_sb", [P, TT, DK // 2], F32)
        id_f = sb("id_f", [P, P], F32)
        id_2 = sb("id_2", [P, DK], F32)
        id_b = sb("id_b", [P, P], BF16)
        mask_b = sb("mask_b", [P, P], BF16)
        gam = sb("gam", [P, KC], F32)
        bet = sb("bet", [P, KC], F32)
        stats = sb("stats", [P, TT, 6], F32)
        mv = sb("mv", [P, TT, 2], F32)
        std = sb("std", [P, TT], F32)
        rstd = sb("rstd", [P, TT], F32)
        nmax_part = sb("nmax_part", [P, 2, 4], F32)
        nmax = sb("nmax", [P, 2], F32)
        rsum = sb("rsum", [P, ROWS, 4], F32)
        rtot = sb("rtot", [P, ROWS], F32)
        rinv = sb("rinv", [P, ROWS], F32)
        pause = sb("pause", [P, 1], F32)

        with ExitStack() as ctx_attn:
            def sba(name, shape, dt):
                return ctx_attn.enter_context(nc.sbuf_tensor(name, shape, dt))

            hn = sba("hn", [P, 2, KC, SEQ], F32R)
            qk_hi = sba("qk_hi", [P, 4, SEQ], F32R)
            k_lo = sba("k_lo", [P, 2, SEQ], F32R)
            v_st = sba("v_st", [P, TT, 2, 2, DK], F32R)
            pt_hi = sba("pt_hi", [P, 2, TT, 2 * P], F32R)
            pt_lo = sba("pt_lo", [P, 2, TT, 2 * P], F32R)
            o_norm = sba("o_norm", [P, TT, P], F32)
            o_sum = sba("o_sum", [P, 2 * P], F32)
            w_hl = sba("w_hl", [P, 2, KC, QKV], F32R)
            w_raw = sba("w_raw", [P, KC, 3, P], F32)
            b_qkv = sba("b_qkv", [P, 3, P], F32)
            qkv_f = [sba(f"qkv_f{i}", [P, 3, DK], F32) for i in range(4)]
            rope_s = sba("rope_s", [P, 2, DK], F32)
            rope_d = [sba(f"rope_d{i}", [P, 2, 2, DK], F32) for i in range(2)]
            probs = sba("probs", [P, 2, SEQ], F32)

        pflat = probs[:, :, :].rearrange("p a n -> p (a n)")
        h_all = pflat.rearrange("p (t d) -> p t d", t=TT)
        onflat = o_norm[:, :, :].rearrange("p t d -> p (t d)")
        hn_f = [onflat[:, 512 * i:512 * (i + 1)] for i in range(2)]

        def split_sb(name, n):
            t = sb(name, [P, 2, n], F32R)
            return [t[:, 0, :], t[:, 1, :]]

        wo_raw = sb("wo_raw", [P, OC * DM], F32)[:, :]
        wg_raw = sb("wg_raw", [P, KC * HID], I32)[:, :]
        wu_raw = sb("wu_raw", [P, KC * HID], I32)[:, :]
        wd_raw = sb("wd_raw", [P, MC * DM], I32)[:, :]
        bo_sb = sb("bo_sb", [P, DM], F32)
        h_g = sb("h_g", [P, TG * DM], F32)[:, :]
        sb("spare_a", [P, 256], F32)

        o_t = split_sb("o_t", OC * 512)
        wo_hl = split_sb("wo_hl", OC * DM)

        wg_hl = split_sb("wg_hl", KC * HID)
        wu_hl = split_sb("wu_hl", KC * HID)
        wd_hl = split_sb("wd_hl", MC * DM)

        x1_t = split_sb("x1_t", KC * 512)
        hid_t = split_sb("hid_t", MC * 512)
        x1_g = sb("x1_g", [P, TG * DM], F32)[:, :]
        x1_keep = sb("x1_keep", [P, TG * DM], F32)[:, :]
        out_g = sb("out_g", [P, TG * DM], F32)[:, :]
        silu_g = [sb(f"silu_g{i}", [P, 512], F32)[:, :] for i in range(2)]
        hid_f = [sb(f"hid_f{i}", [P, 512], F32)[:, :] for i in range(2)]
        ln_stat = sb("ln_stat", [P, TG, 6], F32)
        ln_mv = sb("ln_mv", [P, TG, 2], F32)
        ln_dev = sb("ln_dev", [P, TG], F32)
        ln_inv = sb("ln_inv", [P, TG], F32)
        sb("spare_b", [P, 208], F32)

        o_all = sb("o_all", [P, TG, HEADS * DK], F32)[:, :, :]

        with ExitStack() as ctx_ps:
            s_ps = ctx_ps.enter_context(nc.psum_tensor("s_ps", [P, 4, 512], F32))
            t_ps = ctx_ps.enter_context(nc.psum_tensor("t_ps", [P, 3, 512], F32))
            o_ps = ctx_ps.enter_context(nc.psum_tensor("o_ps", [P, 512], F32))
        s_bank = [s_ps[:, i, :] for i in range(4)]
        gu_ps = ctx.enter_context(nc.psum_tensor("gu_ps", [P, 4, 512], F32))
        y_ps = ctx.enter_context(nc.psum_tensor("y_ps", [P, TG * DM], F32))[:, :]
        z_ps = ctx.enter_context(nc.psum_tensor("z_ps", [P, TG * DM], F32))[:, :]
        gu_bank = [gu_ps[:, i, :] for i in range(4)]
        y_bank = [y_ps[:, 512 * i:512 * (i + 1)] for i in range(2)]

        const_in = sem("const_in")
        primed = sem("primed")
        ones_ready = sem("ones_ready")
        h_in = [sem(f"h_in{g}") for g in range(GROUPS)]
        a_stats = sem("a_stats")
        a_aggr = sem("a_aggr")
        a_eps = sem("a_eps")
        a_std = sem("a_std")
        a_rstd = sem("a_rstd")
        a_norm = sem("a_norm")
        a_turned = sem("a_turned")
        a_affine = sem("a_affine")
        a_hi = sem("a_hi")
        a_lo = sem("a_lo")
        w_in = sem("w_in")
        w_hi = sem("w_hi")
        w_lo = sem("w_lo")
        qkv_done = sem("qkv_done")
        qkv_copied = sem("qkv_copied")
        v_hi = sem("v_hi")
        v_lo = sem("v_lo")
        rope_mul = sem("rope_mul")
        roped = sem("roped")
        b_scaled = sem("b_scaled")
        b_in = [sem(f"b_in{i}") for i in range(2)]
        qk_turned = sem("qk_turned")
        qk_hi_done = sem("qk_hi_done")
        qk_lo_done = sem("qk_lo_done")
        scored = sem("scored")
        max_part = sem("max_part")
        maxed = sem("maxed")
        exped = sem("exped")
        turned = sem("turned")
        p_hi = sem("p_hi")
        p_lo = sem("p_lo")
        pv_done = sem("pv_done")
        o_out = sem("o_out")
        o_turned = sem("o_turned")
        r_sum = sem("r_sum")
        r_inv = sem("r_inv")
        normed = sem("normed")
        o_stored = [sem(f"o_stored{i}") for i in range(2)]
        o_early = sem("o_early")
        wo_in = sem("wo_in")
        cw_in = sem("cw_in")
        bo_in = sem("bo_in")
        hg_in = sem("hg_in")
        x_added = sem("x_added")
        x_kept = sem("x_kept")
        z_added = sem("z_added")
        cw_hi = sem("cw_hi")
        cw_lo = sem("cw_lo")
        o_in = sem("o_in")
        c_turned = sem("c_turned")
        c_hi = sem("c_hi")
        c_lo = sem("c_lo")
        y_done = sem("y_done")
        ln_eps = sem("ln_eps")
        ln_rstd = sem("ln_rstd")
        x_biased = sem("x_biased")
        out_rows = sem("out_rows")
        ln_stats = sem("ln_stats")
        ln_std = sem("ln_std")
        ln_rows = sem("ln_rows")
        x_turned = sem("x_turned")
        x_hi = sem("x_hi")
        x_lo = sem("x_lo")
        gate_up = sem("gate_up")
        silu_done = sem("silu_done")
        hid_done = sem("hid_done")
        hid_hi = sem("hid_hi")
        hid_lo = sem("hid_lo")
        z_done = sem("z_done")
        tile_done = sem("tile_done")
        out_stored = sem("out_stored")

        MUL, TURN_QK, EXP, TURN, PV, FIN = 5, 2, -1, -2, -4, -6
        order = [(0, t) for t in range(TT)] + [(1, t) for t in range(TT)]

        def row(j):
            return order[j % ROWS]

        def row_units(j):
            return [(j, u) for u in range(row(j)[1] // 4 + 1)]

        def width(x):
            return min(4, row(x[0])[1] + 1 - 4 * x[1])

        NU = sum(len(row_units(j)) for j in range(ROWS))
        assert NU % 4 == 0

        def units_to(j):
            return NU * (j // ROWS) + sum(len(row_units(a)) for a in range(j % ROWS + 1))

        def unit_no(x):
            return units_to(x[0] - 1) + x[1]

        NPART = sum(len(row_units(j)) for j in range(ROWS) if len(row_units(j)) > 1)

        def parts_to(j):
            return NPART * (j // ROWS) + sum(len(row_units(a)) for a in range(j % ROWS + 1)
                                             if len(row_units(a)) > 1)

        class Steps:
            def __init__(self, kind):
                self.rows = range(0 if kind == "first" else -ROWS, ROWS if kind == "last" else 2 * ROWS)
                self.steps = range(-MUL if kind == "first" else 0, ROWS - FIN if kind == "last" else ROWS)

            def tile(self, i, stage):
                return [i + stage] if i + stage in self.rows else []

            def units(self, i, stage):
                return row_units(i + stage) if i + stage in self.rows else []

            def couple(self, i, stage):
                return [(i + stage) // 2] if i + stage in self.rows else []

            def final(self, i):
                return self.couple(i, FIN) if i % 2 == 0 else []

        PV_PARTS = [3, 1, 1, 1, 3, 1, 1]

        WEIGHTS_A, WEIGHTS_B, BIAS_A, BIAS_B = TT - 2, 2 * TT - 4, TT + 4, 4

        def early_chunks(seq, i):
            n = 2 * (i - (ROWS + 1))
            return [k for k in (n, n + 1) if seq is LAST and 0 <= k < OC]

        FIRST, MIDDLE, LAST = Steps("first"), Steps("middle"), Steps("last")

        ring = []
        for i in range(ROWS):
            tr = [("turn",) + x for x in MIDDLE.units(i, TURN)]
            ring += tr[1:2] + [("mul", i + MUL, 0)] + tr[2:3] + [("qk", i + TURN_QK, 0)] + tr[3:4]
            ring += [("out", 2 * c, 0) for c in MIDDLE.final(i)] + [("turn", i + EXP, 0)]
        while len(ring) % 3:
            ring.append(None)
        slots = {x: n for n, x in enumerate(ring) if x}
        ring_step = {"turn": -TURN, "out": -FIN, "mul": -MUL, "qk": -TURN_QK}

        def step_of(x):
            return x[1] + ring_step[x[0]] - (x[0] == "turn" and x[2] == 0)

        def last_scored_late(units):
            return len(units) >= 2

        def slot(x):
            kind, j, u = x
            pairs = step_of(x) // ROWS
            return slots[(kind, j - pairs * ROWS, u)] + pairs * len(ring)

        def bank(kind, j, u=0):
            return t_ps[:, slot((kind, j, u)) % 3, :]

        def use_before(seq, x):
            n = slot(x) - 3
            while True:
                pairs, y = n // len(ring), ring[n % len(ring)]
                if y is not None:
                    y = (y[0], y[1] + pairs * ROWS, y[2])
                    if y[1] in seq.rows:
                        return y
                    if step_of(y) < seq.steps[0]:
                        return None
                n -= 3

        block = ctx.enter_context(nc.Block())

        @block.sync
        def _(sp):
            def load_input(batch):
                for g in range(GROUPS):
                    sp.dma_start(h_all[:, TG * g:TG * (g + 1), :],
                                 h[bass.ds(batch, 1), g * TG * P:(g + 1) * TG * P, :]
                                 .rearrange("a (t p) d -> p (a t) d", p=P)).then_inc(h_in[g], 16)

            load_input(0)
            for dst, src in ((cos_sb[:, :, :], cos), (sin_sb[:, :, :], sin), (id_f[:, :], ident),
                             (id_2[:, :], ident2), (id_b[:, :], mask[0]), (mask_b[:, :], mask[1]),
                             (gam[:, :], gamma),
                             (bet[:, :], beta)):
                sp.dma_start(dst, src).then_inc(const_in, 16)
            sp.wait_ge(primed, 1)

            def load_w(cols):
                for j in range(3):
                    sp.dma_start(w_raw[:, :, j, :],
                                 wqkv[j, :, bass.ds(cols, P)].rearrange("(k p) n -> p k n", p=P)).then_inc(w_in, 16)

            def load_b(head, cols):
                here = slice(head * DK, (head + 1) * DK)
                for j in range(3):
                    sp.dma_start(b_qkv[:, j, here],
                                 bqkv[j, bass.ds(cols, DK)].partition_broadcast(P)).then_inc(b_in[head], 16)

            def load_first():
                load_w(0)
                load_b(0, 0)
                load_b(1, DK)

            load_first()
            with sp.Fori(0, BATCH) as b:
                def load_ffn(dst, src, k, done):
                    sp.dma_start(dst.rearrange("p (k n) -> p k n", k=k),
                                 src.rearrange("(k p) n -> p k n", p=P)).then_inc(done, 16)

                def load_o(rows):
                    sp.dma_start(o_all, attn[bass.ds(b, 1), bass.ds(rows, TG * P), :]
                                 .rearrange("a (t p) n -> p (a t) n", p=P)).then_inc(o_in, 16)

                def load_h(rows):
                    sp.dma_start(h_g.rearrange("p (t d) -> p t d", t=TG),
                                 h[bass.ds(b, 1), bass.ds(rows, TG * P), :]
                                 .rearrange("a (t p) d -> p (a t) d", p=P)).then_inc(hg_in, 16)

                def store_attn(head, cols, t0, t1, done):
                    sp.dma_start(attn[bass.ds(b, 1), t0 * P:t1 * P, bass.ds(cols, DK)]
                                 .rearrange("a (t p) n -> p (a t) n", p=P),
                                 o_norm[:, t0:t1, head * DK:(head + 1) * DK]).then_inc(done, 16)

                def store_out(rows):
                    sp.dma_start(out[bass.ds(b, 1), bass.ds(rows, TG * P), :]
                                 .rearrange("a (t p) d -> p (a t) d", p=P),
                                 out_g.rearrange("p (t d) -> p t d", t=TG)).then_inc(out_stored, 16)

                def pair(pr, last):
                    it = b * PAIRS + pr
                    split = sp.snap(it * 4 + 4)
                    biases_used = [sp.snap(it * ROWS + TT), sp.snap(it * ROWS + 2 * TT)]
                    divided = [sp.snap(it * COUPLES + COUPLES // 2), sp.snap(it * COUPLES + COUPLES)]
                    cols = [sp.snap(pr * P), sp.snap(pr * P + DK)]
                    next_cols = [sp.snap(pr * P + P), sp.snap(pr * P + (P + DK))]
                    all_stored = sp.snap(b * (16 * PAIRS) + (16 * PAIRS + 16))
                    v_split, all_turned = sp.snap(it * ROWS + (ROWS + 4)), sp.snap(it * ROWS + (ROWS + 2))
                    early, early_stored = sp.snap(it * COUPLES + (COUPLES + TG) // 2), sp.snap(b * 16 + 16)
                    if not last:
                        sp.wait_ge(w_lo, split)
                        load_w(next_cols[0])
                    for head in range(2):
                        if not last:
                            sp.wait_ge(qkv_copied, biases_used[head])
                            load_b(head, next_cols[head])
                        elif head == 1:
                            sp.wait_ge(v_lo, v_split)
                            load_ffn(wo_raw, wo, OC, wo_in)
                            sp.wait_ge(qk_turned, all_turned)
                            load_ffn(wg_raw, wgate_t, KC, cw_in)
                            sp.wait_ge(o_stored[0], all_stored)
                            load_ffn(wu_raw, wup_t, KC, cw_in)
                            load_h(0)
                            sp.wait_ge(normed, early)
                            store_attn(head, cols[head], 0, TG, o_early)
                            sp.wait_ge(o_early, early_stored)
                            sp.dma_start(bo_sb[:, :], bo.partition_broadcast(P)).then_inc(bo_in, 16)
                            load_o(0)
                        sp.wait_ge(normed, divided[head])
                        store_attn(head, cols[head], TG if last and head == 1 else 0, TT, o_stored[head])

                with sp.Fori(0, PAIRS - 1) as pr:
                    pair(pr, False)
                pair(PAIRS - 1, True)
                all_stored = sp.snap(b * (16 * PAIRS) + (16 * PAIRS + 16))
                sp.wait_ge(o_stored[1], all_stored)
                load_ffn(wd_raw, wdown_t, MC, cw_in)
                with sp.Fori(0, GROUPS - 1) as g:
                    c = b * GROUPS + g
                    turned_o, added = sp.snap(c * OC + OC), sp.snap(c + 1)
                    next_rows = sp.snap(g * (TG * P) + TG * P)
                    sp.wait_ge(c_turned, turned_o)
                    load_o(next_rows)
                    sp.wait_ge(x_added, added)
                    load_h(next_rows)
                assert BATCH == 2
                load_input(1 - b)
                with sp.Fori(0, GROUPS - 1) as g:
                    done, rows = sp.snap(b * GROUPS + g + 2), sp.snap(g * (TG * P))
                    sp.wait_ge(tile_done, done)
                    store_out(rows)
                last_done = sp.snap(b * GROUPS + (GROUPS + 1))
                load_first()
                sp.wait_ge(tile_done, last_done)
                store_out((GROUPS - 1) * TG * P)
            sp.wait_ge(w_in, 48 * (BATCH * PAIRS + 1))
            for head in range(2):
                sp.wait_ge(b_in[head], 48 * (BATCH * PAIRS + 1))
            sp.wait_ge(o_early, 16 * BATCH)
            sp.wait_ge(out_stored, 16 * BATCH * GROUPS + 16)
            for head in range(2):
                sp.wait_ge(o_stored[head], 16 * BATCH * PAIRS + 16)

        @block.gpsimd
        def _(pool):
            pool.wait_ge(const_in, 16 * 8)
            def tile(n, head, t):
                x = qkv_f[t % 4]
                pool.wait_ge(qkv_copied, n + 1)
                pool.wait_ge(roped, 2 * n + 8)
                x4 = x[:, 0:2, :].rearrange("p v (a d) -> p (v a) d", a=2)
                nc.gpsimd.tensor_tensor(rope_s[:, :, :].rearrange("p v (a d) -> p (v a) d", a=2), x4,
                                        sin_sb[:, t, :].unsqueeze(1).broadcast_to([P, 4, DK // 2]),
                                        ALU.mult).then_inc(rope_mul, 1)
                pool.wait_ge(rope_mul, 2 * n + 1)
                nc.gpsimd.tensor_tensor(x4, x4, cos_sb[:, t, :].unsqueeze(1).broadcast_to([P, 4, DK // 2]),
                                        ALU.mult).then_inc(rope_mul, 1)
                pool.wait_ge(rope_mul, 2 * n + 2)
                pool.wait_ge(qk_turned, n + 1)
                half = DK // 2
                for a, op in ((0, ALU.subtract), (1, ALU.add)):
                    c = x[:, 0:2, a * half:(a + 1) * half].unsqueeze(2).broadcast_to([P, 2, 2, half])
                    s = rope_s[:, :, (1 - a) * half:(2 - a) * half].unsqueeze(2).broadcast_to([P, 2, 2, half])
                    nc.gpsimd.tensor_tensor(rope_d[t % 2][:, :, :, a * half:(a + 1) * half], c, s, op)\
                      .then_inc(roped, 1)
                pool.wait_ge(v_hi, n + 1)
                nc.gpsimd.tensor_tensor(v_st[:, t, head, 1, :], x[:, 2, :], v_st[:, t, head, 0, :].bitcast(F32),
                                        ALU.subtract).then_inc(v_lo, 1)

            with pool.Fori(0, BATCH * PAIRS) as it:
                for j in range(ROWS):
                    head, t = row(j)
                    tile(it * ROWS + j, head, t)

        @block.scalar
        def _(act):
            act.wait_ge(const_in, 16 * 8)
            act.wait_ge(primed, 1)

            def root_input(n):
                act.wait_ge(a_eps, n + 1)
                nc.scalar.activation(std[:, :], mv[:, :, 1], ACT.Sqrt).then_inc(a_std, 1)

            root_input(0)
            with act.Fori(0, BATCH) as b:
                def weights(n, head):
                    act.wait_ge(w_in, n * 48 + 48)
                    wh = w_hl[:, 0, :, :].rearrange("p k (j n) -> p k j n", j=3)
                    here = slice(head * DK, (head + 1) * DK)
                    nc.scalar.activation(wh[:, :, 0, here], w_raw[:, :, 0, here], ACT.Copy, scale=SCALE)\
                      .then_inc(w_hi, 1)
                    nc.scalar.activation(wh[:, :, 1:3, here], w_raw[:, :, 1:3, here], ACT.Copy).then_inc(w_hi, 1)

                def bias(n, head):
                    act.wait_ge(b_in[head], n * 48 + 48)
                    here = slice(head * DK, (head + 1) * DK)
                    nc.scalar.activation(b_qkv[:, 0, here], b_qkv[:, 0, here], ACT.Copy, scale=SCALE)\
                      .then_inc(b_scaled, 1)

                def attn_hi(c, k, banks):
                    act.wait_ge(c_turned, c * OC + (k + 1))
                    nc.scalar.activation(o_t[0][:, 512 * k:512 * (k + 1)], banks[k % len(banks)], ACT.Copy)\
                      .then_inc(c_hi, 1)

                def run(seq, it):
                    def copy_v(j):
                        head, t = row(j)
                        act.wait_ge(qkv_copied, it * ROWS + (j + 1))
                        nc.scalar.activation(v_st[:, t, head, 0, :], qkv_f[j % 4][:, 2, :], ACT.Copy).then_inc(v_hi, 1)

                    def qk_hi_part(j):
                        head, t = row(j)
                        act.wait_ge(qk_turned, it * ROWS + (j + 3))
                        nc.scalar.activation(qk_hi[:, head:4:2, t * P:(t + 1) * P],
                                             bank("qk", j)[:, 0:2 * P].rearrange("p (v n) -> p v n", v=2), ACT.Copy)\
                          .then_inc(qk_hi_done, 1)

                    def hi_part(x):
                        j, u = x
                        n, t = width(x), row(j)[1]
                        if j - 4 in seq.rows:
                            act.wait_ge(pv_done, it * COUPLES + (j // 2 - 1))
                        act.wait_ge(turned, it * NU + (unit_no(x) + 1))
                        nc.scalar.activation(
                            pt_hi[:, (j // 2) % 2, 4 * u:4 * u + n, (t % 2) * P:(t % 2 + 1) * P],
                            bank("turn", j, u)[:, 0:n * P].rearrange("p (k q) -> p k q", k=n), ACT.Copy)\
                          .then_inc(p_hi, 1)

                    def exp_part(x):
                        j, u = x
                        head, t = row(j)
                        w = width(x) * P
                        act.wait_ge(maxed, it * ROWS + (j + 1))
                        if j - 2 in seq.rows and u == 0:
                            act.wait_ge(turned, it * NU + units_to(j - 2))
                        nc.scalar.activation(probs[:, j % 2, 512 * u:512 * u + w],
                                             s_bank[unit_no(x) % 4][:, 0:w], ACT.Exp,
                                             bias=nmax[:, j % 2:j % 2 + 1],
                                             accum_out=rsum[:, head * TT + t, u:u + 1]).then_inc(exped, 1)

                    def copy_out(c):
                        act.wait_ge(pv_done, it * COUPLES + (c + 1))
                        if 2 * c - 2 in seq.rows:
                            act.wait_ge(o_turned, it * COUPLES + c)
                        nc.scalar.activation(o_sum[:, :], o_ps[:, 0:2 * P], ACT.Copy).then_inc(o_out, 1)

                    for i in seq.steps:
                        tr, ex = seq.units(i, TURN), seq.units(i, EXP)
                        for k in range(4):
                            for x in (tr[0:2] if k == 0 else tr[k:k + 1] if k >= 2 else []):
                                hi_part(x)
                            for x in ex[k:k + 1]:
                                exp_part(x)
                            if k == 2:
                                for j in seq.tile(i, TURN_QK):
                                    qk_hi_part(j)
                            if k == 0:
                                for j in seq.tile(i, MUL - 1):
                                    copy_v(j)
                        if i % 2 == 1:
                            for c in seq.couple(i, PV):
                                copy_out(c)
                        chunks = early_chunks(seq, i)
                        if 0 in chunks:
                            act.wait_ge(wo_in, b * 16 + 16)
                            nc.scalar.activation(wo_hl[0], wo_raw, ACT.Copy).then_inc(cw_hi, 1)
                        for k in chunks:
                            attn_hi(b * GROUPS, k, gu_bank)
                        if i == BIAS_B:
                            bias(it, 1)
                        if seq is not LAST:
                            if i == WEIGHTS_A:
                                act.wait_ge(qkv_done, it * ROWS + TT)
                                weights(it + 1, 0)
                            if i == WEIGHTS_B:
                                act.wait_ge(qkv_done, it * ROWS + 2 * TT)
                                weights(it + 1, 1)
                            if i == BIAS_A:
                                bias(it + 1, 0)

                for head in range(2):
                    weights(b * PAIRS, head)
                bias(b * PAIRS, 0)
                for i in range(KC * GROUPS):
                    k, g = i // GROUPS, i % GROUPS
                    act.wait_ge(a_turned, b * 8 + (i + 1))
                    if i >= 2:
                        act.wait_ge(a_lo, b * 8 + (i - 1))
                    nc.scalar.activation(hn_f[i % 2], s_bank[i % 4], ACT.Identity,
                                         bias=bet[:, k:k + 1], scale=gam[:, k:k + 1]).then_inc(a_affine, 1)
                    act.wait_ge(a_affine, b * 8 + (i + 1))
                    nc.scalar.activation(hn[:, 0, k, 512 * g:512 * (g + 1)], hn_f[i % 2], ACT.Copy)\
                      .then_inc(a_hi, 1)
                run(FIRST, b * PAIRS)
                with act.Fori(1, PAIRS - 1) as pr:
                    run(MIDDLE, b * PAIRS + pr)
                run(LAST, b * PAIRS + (PAIRS - 1))

                act.wait_ge(cw_in, b * 48 + 48)
                for dst, raw in ((wg_hl, wg_raw), (wu_hl, wu_raw), (wd_hl, wd_raw)):
                    nc.scalar.activation(dst[0], raw, ACT.Copy).then_inc(cw_hi, 1)

                def root(n):
                    act.wait_ge(ln_eps, n + 1)
                    nc.scalar.activation(ln_dev[:, :], ln_mv[:, :, 1], ACT.Sqrt).then_inc(ln_std, 1)

                def ffn_hi(c, turns):
                    act.wait_ge(ln_rows, c * TG + TG)
                    nc.scalar.activation(x1_keep, x1_g, ACT.Copy).then_inc(x_kept, 1)
                    for k in range(KC):
                        act.wait_ge(x_turned, c * KC + (k + 1))
                        nc.scalar.activation(x1_t[0][:, 512 * k:512 * (k + 1)], gu_bank[k], ACT.Copy)\
                          .then_inc(x_hi, 1)
                    for m in range(MC + 1):
                        if m < MC:
                            act.wait_ge(gate_up, c * MC + (m + 1))
                            if m >= 2:
                                act.wait_ge(hid_done, c * MC + (m - 1))
                            nc.scalar.activation(silu_g[m % 2], gu_bank[2 - 2 * (m % 2)], ACT.Silu, scale=DEQ)\
                              .then_inc(silu_done, 1)
                        if m >= 1:
                            act.wait_ge(hid_done, c * MC + m)
                            nc.scalar.activation(hid_t[0][:, 512 * (m - 1):512 * m], hid_f[(m - 1) % 2], ACT.Copy)\
                              .then_inc(hid_hi, 1)
                        if turns and m < MC:
                            attn_hi(c + 2, m, y_bank)
                    if turns:
                        for k in range(MC, OC):
                            attn_hi(c + 2, k, y_bank)

                for k in range(OC):
                    attn_hi(b * GROUPS + 1, k, gu_bank)
                root(b * (2 * GROUPS))
                with act.Fori(0, GROUPS - 2) as g:
                    c = b * GROUPS + g
                    ffn_hi(c, True)
                    root(c * 2 + 1)
                    root(c * 2 + 2)
                c = b * GROUPS + (GROUPS - 2)
                ffn_hi(c, False)
                root_input(b + 1)
                root(c * 2 + 1)
                root(c * 2 + 2)
                ffn_hi(c + 1, False)
                root(c * 2 + 3)

        @block.vector
        def _(dve):
            nc.vector.memset(rsum[:, :, :], 0.0).then_inc(ones_ready, 1)
            nc.vector.memset(rstd[:, 0:1], 0.0).then_inc(qk_turned, 2)
            nc.vector.memset(rstd[:, 1:2], 0.0).then_inc(v_lo, 4)
            nc.vector.memset(rstd[:, 2:3], 0.0).then_inc(roped, 8)
            nc.vector.memset(nmax[:, 1:2], 0.0).then_inc(tile_done, 1)
            nc.vector.memset(rinv[:, :], 0.0).then_inc(out_stored, 16)
            nc.vector.memset(rtot[:, 0:8], 0.0).then_inc(o_stored[0], 16)
            nc.vector.memset(rtot[:, 8:16], 0.0).then_inc(o_stored[1], 16)
            nc.vector.memset(pause[:, :], 0.0).then_inc(z_added, 1)
            nc.vector.memset(rtot[:, 16:32], 0.0).then_inc(primed, 1)

            def input_stats(n, t):
                if t % TG == 0:
                    dve.wait_ge(h_in[t // TG], n * 16 + 16)
                nc.vector.bn_stats(stats[:, t, :], h_all[:, t, :]).then_inc(a_stats, 1)

            def input_var(n):
                dve.wait_ge(a_stats, n * TT + TT)
                nc.vector.memset(pause[:, :], 0.0).then_inc(a_aggr, 1)
                for t in range(TT):
                    nc.vector.bn_aggr(mv[:, t, :], stats[:, t, :]).then_inc(a_aggr, 1)
                dve.wait_ge(a_aggr, n * (TT + 1) + (TT + 1))
                nc.vector.tensor_scalar(mv[:, :, 1], mv[:, :, 1], EPS, None, ALU.add).then_inc(a_eps, 1)

            def input_inv(n):
                dve.wait_ge(a_std, n + 1)
                nc.vector.reciprocal(rstd[:, :], std[:, :]).then_inc(a_rstd, 1)

            def input_rows(n, t):
                if t == 0:
                    dve.wait_ge(a_rstd, n + 1)
                nc.vector.tensor_scalar(h_all[:, t, :], h_all[:, t, :], mv[:, t, 0:1], rstd[:, t:t + 1],
                                        ALU.subtract, ALU.mult).then_inc(a_norm, 1)

            for t in range(TT):
                input_stats(0, t)
            input_var(0)
            input_inv(0)
            for t in range(TT):
                input_rows(0, t)
            with dve.Fori(0, BATCH) as b:
                def weights(n, head):
                    dve.wait_ge(w_in, n * 48 + 48)
                    dve.wait_ge(w_hi, n * 4 + (2 * head + 2))
                    wv = w_hl[:, :, :, :].rearrange("p a k (j n) -> p a k j n", j=3)
                    here = slice(head * DK, (head + 1) * DK)
                    nc.vector.scalar_tensor_tensor(
                        wv[:, 1, :, 0, here], w_raw[:, :, 0, here], SCALE, wv[:, 0, :, 0, here].bitcast(F32),
                        ALU.mult, ALU.subtract).then_inc(w_lo, 1)
                    nc.vector.tensor_tensor(
                        wv[:, 1, :, 1:3, here], w_raw[:, :, 1:3, here], wv[:, 0, :, 1:3, here].bitcast(F32),
                        ALU.subtract).then_inc(w_lo, 1)

                def attn_lo(c, k, banks):
                    dve.wait_ge(c_hi, c * OC + (k + 1))
                    nc.vector.tensor_tensor(o_t[1][:, 512 * k:512 * (k + 1)], banks[k % len(banks)],
                                            o_t[0][:, 512 * k:512 * (k + 1)].bitcast(F32), ALU.subtract)\
                      .then_inc(c_lo, 1)

                def split_weights(n, dst, raw):
                    dve.wait_ge(cw_hi, b * 4 + (n + 1))
                    nc.vector.tensor_tensor(dst[1], raw, dst[0].bitcast(F32), ALU.subtract).then_inc(cw_lo, 1)

                def run(seq, it):
                    def qk_lo_part(j):
                        head, t = row(j)
                        here = slice(t * P, (t + 1) * P)
                        src = bank("qk", j)
                        dve.wait_ge(qk_hi_done, it * ROWS + (j + 1))
                        nc.vector.tensor_tensor(k_lo[:, head, here], src[:, P:2 * P],
                                                qk_hi[:, 2 + head, here].bitcast(F32), ALU.subtract)\
                          .then_inc(qk_lo_done, 1)
                        nc.vector.tensor_tensor(qk_hi[DK:P, head, here], src[DK:P, 0:P],
                                                qk_hi[DK:P, head, here].bitcast(F32), ALU.subtract)\
                          .then_inc(qk_lo_done, 1)

                    def copy_qkv(j):
                        head, t = row(j)
                        n = it * ROWS + j
                        if t == 0:
                            dve.wait_ge(b_scaled, it * 2 + (2 * (j // ROWS) + head + 1))
                        dve.wait_ge(qkv_done, n + 1)
                        dve.wait_ge(v_lo, n + 1)
                        dve.wait_ge(roped, n * 2 + 2)
                        nc.vector.tensor_tensor(
                            qkv_f[j % 4][:, :, :], bank("mul", j)[:, 0:3 * DK].rearrange("p (j d) -> p j d", j=3),
                            b_qkv[:, :, head * DK:(head + 1) * DK], ALU.add).then_inc(qkv_copied, 1)

                    def unit_max(x):
                        j, u = x
                        n = len(row_units(j))
                        if j - 2 in seq.rows and u == 0:
                            dve.wait_ge(exped, it * NU + units_to(j - 2))
                        dve.wait_ge(scored, it * NU + (unit_no(x) + 1))
                        scores = s_bank[unit_no(x) % 4][:, 0:width(x) * P]
                        if n == 1:
                            nc.vector.tensor_reduce(nmax[:, j % 2:j % 2 + 1], scores, AX.X, ALU.max, negate=True)\
                              .then_inc(maxed, 1)
                            return
                        nc.vector.tensor_reduce(nmax_part[:, j % 2, u:u + 1], scores, AX.X, ALU.max, negate=True)\
                          .then_inc(max_part, 1)
                        if u == n - 1:
                            dve.wait_ge(max_part, it * NPART + parts_to(j))
                            nc.vector.tensor_reduce(nmax[:, j % 2:j % 2 + 1], nmax_part[:, j % 2, 0:n],
                                                    AX.X, ALU.min).then_inc(maxed, 1)

                    def lo_part(x):
                        j, u = x
                        n, t = width(x), row(j)[1]
                        dve.wait_ge(p_hi, it * NU + (unit_no(x) + 1))
                        here = (slice(None), (j // 2) % 2, slice(4 * u, 4 * u + n),
                                slice((t % 2) * P, (t % 2 + 1) * P))
                        nc.vector.tensor_tensor(
                            pt_lo[here], bank("turn", j, u)[:, 0:n * P].rearrange("p (k q) -> p k q", k=n),
                            pt_hi[here].bitcast(F32), ALU.subtract).then_inc(p_lo, 1)

                    def invert(c):
                        head, t = row(2 * c)
                        rows = slice(head * TT + t, head * TT + t + 2)
                        nc.vector.tensor_reduce(rtot[:, rows], rsum[:, rows, :], AX.X, ALU.add).then_inc(r_sum, 1)
                        dve.wait_ge(r_sum, it * COUPLES + (c + 1))
                        nc.vector.reciprocal(rinv[:, rows], rtot[:, rows]).then_inc(r_inv, 1)

                    def divide(c):
                        head, t = row(2 * c)
                        rows = slice(head * TT + t, head * TT + t + 2)
                        if t == 0:
                            dve.wait_ge(o_stored[head], it * 16 + 16)
                        dve.wait_ge(o_turned, it * COUPLES + (c + 1))
                        dve.wait_ge(r_inv, it * COUPLES + (c + 1))
                        nc.vector.tensor_tensor(
                            o_norm[:, t:t + 2, head * DK:(head + 1) * DK],
                            bank("out", 2 * c)[:, 0:2 * DK].rearrange("p (a d) -> p a d", a=2),
                            rinv[:, rows].unsqueeze(2).broadcast_to([P, 2, DK]), ALU.mult).then_inc(normed, 1)

                    for i in seq.steps:
                        tr, sc = seq.units(i, TURN), seq.units(i, 0)
                        late = sc[-1:] if last_scored_late(sc) else []
                        for k in range(4):
                            for x in (tr[0:2] if k == 0 else tr[k + 1:k + 2]):
                                lo_part(x)
                            if k == 0:
                                for j in seq.tile(i, MUL):
                                    copy_qkv(j)
                            for x in sc[k:k + 1]:
                                if x not in late:
                                    unit_max(x)
                            if k == 1:
                                for j in seq.tile(i, TURN_QK):
                                    qk_lo_part(j)
                            if k == 2:
                                for c in seq.final(i):
                                    divide(c)
                        for x in late:
                            unit_max(x)
                        if i % 2 == 0:
                            for c in seq.couple(i, PV):
                                invert(c)
                        chunks = early_chunks(seq, i)
                        if 0 in chunks:
                            split_weights(0, wo_hl, wo_raw)
                        for k in chunks:
                            attn_lo(b * GROUPS, k, gu_bank)
                        if seq is not LAST:
                            if i == WEIGHTS_A:
                                weights(it + 1, 0)
                            if i == WEIGHTS_B:
                                weights(it + 1, 1)

                for head in range(2):
                    weights(b * PAIRS, head)
                dve.wait_ge(out_stored, b * (16 * GROUPS) + 16)
                for i in range(KC * GROUPS):
                    k, g = i // GROUPS, i % GROUPS
                    dve.wait_ge(a_hi, b * 8 + (i + 1))
                    nc.vector.tensor_tensor(hn[:, 1, k, 512 * g:512 * (g + 1)], hn_f[i % 2],
                                            hn[:, 0, k, 512 * g:512 * (g + 1)].bitcast(F32), ALU.subtract)\
                      .then_inc(a_lo, 1)
                run(FIRST, b * PAIRS)
                with dve.Fori(1, PAIRS - 1) as pr:
                    run(MIDDLE, b * PAIRS + pr)
                run(LAST, b * PAIRS + (PAIRS - 1))

                for n, (dst, raw) in enumerate(((wg_hl, wg_raw), (wu_hl, wu_raw), (wd_hl, wd_raw))):
                    split_weights(n + 1, dst, raw)

                def norm(x, n, rows_done):
                    for t in range(TG):
                        nc.vector.bn_stats(ln_stat[:, t, :], x[:, t * DM:(t + 1) * DM]).then_inc(ln_stats, 1)
                    dve.wait_ge(ln_stats, n * (2 * TG + 1) + TG)
                    nc.vector.memset(pause[:, :], 0.0).then_inc(ln_stats, 1)
                    for t in range(TG):
                        nc.vector.bn_aggr(ln_mv[:, t, :], ln_stat[:, t, :]).then_inc(ln_stats, 1)
                    dve.wait_ge(ln_stats, n * (2 * TG + 1) + (2 * TG + 1))
                    nc.vector.tensor_scalar(ln_mv[:, :, 1], ln_mv[:, :, 1], EPS, None, ALU.add).then_inc(ln_eps, 1)
                    dve.wait_ge(ln_std, n + 1)
                    nc.vector.reciprocal(ln_inv[:, :], ln_dev[:, :]).then_inc(ln_rstd, 1)
                    dve.wait_ge(ln_rstd, n + 1)
                    for t in range(TG):
                        nc.vector.tensor_scalar(x[:, t * DM:(t + 1) * DM], x[:, t * DM:(t + 1) * DM],
                                                ln_mv[:, t, 0:1], ln_inv[:, t:t + 1],
                                                ALU.subtract, ALU.mult).then_inc(rows_done, 1)

                def add_residual(c, first):
                    dve.wait_ge(hg_in, c * 16 + 16)
                    dve.wait_ge(y_done, c + 1)
                    if not first:
                        dve.wait_ge(x_kept, c)
                        dve.wait_ge(x_turned, c * KC)
                    nc.vector.scalar_tensor_tensor(x1_g, h_g, 2.0, y_ps, ALU.mult, ALU.add).then_inc(x_added, 1)

                def first_norm(c, n, first):
                    dve.wait_ge(x_added, c + 1)
                    if first:
                        dve.wait_ge(bo_in, b * 16 + 16)
                    x3 = x1_g.rearrange("p (t d) -> p t d", t=TG)
                    nc.vector.tensor_tensor(x3, x3, bo_sb[:, :].unsqueeze(1).broadcast_to([P, TG, DM]),
                                            ALU.add).then_inc(x_biased, 1)
                    dve.wait_ge(x_biased, c + 1)
                    norm(x1_g, n, ln_rows)

                def ffn_lo(c):
                    for k in range(KC):
                        dve.wait_ge(x_hi, c * KC + (k + 1))
                        nc.vector.tensor_tensor(x1_t[1][:, 512 * k:512 * (k + 1)], gu_bank[k],
                                                x1_t[0][:, 512 * k:512 * (k + 1)].bitcast(F32), ALU.subtract)\
                          .then_inc(x_lo, 1)

                def ffn_hidden(c, turns, also=lambda m: None):
                    for m in range(MC + 1):
                        if m < MC:
                            dve.wait_ge(silu_done, c * MC + (m + 1))
                            if m >= 2:
                                dve.wait_ge(hid_hi, c * MC + (m - 1))
                                dve.wait_ge(hid_lo, c * MC + (m - 1))
                            nc.vector.scalar_tensor_tensor(hid_f[m % 2], gu_bank[3 - 2 * (m % 2)], DEQ,
                                                           silu_g[m % 2], ALU.mult, ALU.mult).then_inc(hid_done, 1)
                        if m >= 1:
                            dve.wait_ge(hid_hi, c * MC + m)
                            nc.vector.tensor_tensor(hid_t[1][:, 512 * (m - 1):512 * m], hid_f[(m - 1) % 2],
                                                    hid_t[0][:, 512 * (m - 1):512 * m].bitcast(F32), ALU.subtract)\
                              .then_inc(hid_lo, 1)
                        if m < MC:
                            if turns:
                                attn_lo(c + 2, m, y_bank)
                            also(m)
                    if turns:
                        for k in range(MC, OC):
                            attn_lo(c + 2, k, y_bank)

                def second_norm(c, n):
                    dve.wait_ge(z_done, c + 1)
                    dve.wait_ge(x_kept, c + 1)
                    dve.wait_ge(out_stored, c * 16 + 16)
                    nc.vector.scalar_tensor_tensor(out_g, z_ps, DEQ, x1_keep, ALU.mult, ALU.add)\
                      .then_inc(z_added, 1)
                    dve.wait_ge(z_added, c + 2)
                    norm(out_g, n, out_rows)
                    dve.wait_ge(out_rows, c * TG + TG)
                    nc.vector.memset(pause[:, :], 0.0).then_inc(tile_done, 1)

                def share(m):
                    return range(m * TT // MC, (m + 1) * TT // MC)

                c = b * GROUPS
                add_residual(c, True)
                for k in range(OC):
                    attn_lo(c + 1, k, gu_bank)
                first_norm(c, c * 2, True)
                with dve.Fori(0, GROUPS - 2) as g:
                    c = b * GROUPS + g
                    ffn_lo(c)
                    add_residual(c + 1, False)
                    ffn_hidden(c, True)
                    first_norm(c + 1, c * 2 + 1, False)
                    second_norm(c, c * 2 + 2)
                c = b * GROUPS + (GROUPS - 2)
                ffn_lo(c)
                add_residual(c + 1, False)
                ffn_hidden(c, False, lambda m: [input_stats(b + 1, t) for t in share(m)])
                input_var(b + 1)
                first_norm(c + 1, c * 2 + 1, False)
                input_inv(b + 1)
                second_norm(c, c * 2 + 2)
                ffn_lo(c + 1)
                ffn_hidden(c + 1, False, lambda m: [input_rows(b + 1, t) for t in share(m)])
                second_norm(c + 1, c * 2 + 3)

        @block.tensor
        def _(pe):
            def product(dst, lhs, rhs, first=True, last=True):
                nc.tensor.matmul(dst, lhs[0], rhs[0], start=first, stop=False)
                nc.tensor.matmul(dst, lhs[1], rhs[0], start=False, stop=False)
                return nc.tensor.matmul(dst, lhs[0], rhs[1], start=False, stop=last)

            pe.wait_ge(const_in, 16 * 8)
            pe.wait_ge(ones_ready, 1)
            pe.wait_ge(primed, 1)
            with pe.Fori(0, BATCH) as b:
                for i in range(KC * GROUPS):
                    k, g = i // GROUPS, i % GROUPS
                    if k == 0:
                        pe.wait_ge(a_norm, b * TT + 4 * (g + 1))
                    if i == 0:
                        pe.wait_ge(z_added, b * GROUPS + 1)
                    if i >= 4:
                        pe.wait_ge(a_affine, b * 8 + (i - 3))
                    for j in range(4):
                        last = nc.tensor.transpose(s_bank[i % 4][:, j * P:(j + 1) * P],
                                                   h_all[:, 4 * g + j, k * P:(k + 1) * P], id_f[:, :])
                    last.then_inc(a_turned, 1)

                def turn_attn(c, k, banks):
                    if k == 0:
                        pe.wait_ge(o_in, c * 16 + 16)
                    if k >= len(banks):
                        pe.wait_ge(c_lo, c * OC + (k + 1 - len(banks)))
                    for t in range(TG):
                        last = nc.tensor.transpose(banks[k % len(banks)][:, t * P:(t + 1) * P],
                                                   o_all[:, t, k * P:(k + 1) * P], id_f[:, :])
                    last.then_inc(c_turned, 1)

                def run(seq, it):
                    def ring_free(kind, j, u=0):
                        y = use_before(seq, (kind, j, u))
                        if y is None:
                            return
                        kind, j, u = y
                        if kind == "turn":
                            pe.wait_ge(p_lo, it * NU + (unit_no((j, u)) + 1))
                        elif kind == "out":
                            pe.wait_ge(normed, it * COUPLES + (j // 2 + 1))
                        elif kind == "mul":
                            pe.wait_ge(qkv_copied, it * ROWS + (j + 1))
                        else:
                            pe.wait_ge(qk_lo_done, it * (2 * ROWS) + (2 * j + 2))

                    def multiply(j):
                        head, t = row(j)
                        ring_free("mul", j)
                        if t == 0:
                            pe.wait_ge(w_lo, it * 4 + (4 * (j // ROWS) + 2 * head + 2))
                        here = slice(t * P, (t + 1) * P)
                        for k in range(KC):
                            last = product(bank("mul", j)[:, 0:3 * DK], [hn[:, a, k, here] for a in range(2)],
                                           [w_hl[:, a, k, :].rearrange("p (j h d) -> p j h d", j=3, h=2)[:, :, head, :]
                                            for a in range(2)], first=(k == 0), last=(k == KC - 1))
                        last.then_inc(qkv_done, 1)

                    def turn_qk(j):
                        ring_free("qk", j)
                        pe.wait_ge(roped, it * (2 * ROWS) + (2 * j + 10))
                        for v in range(2):
                            last = nc.tensor.transpose(bank("qk", j)[:, v * P:(v + 1) * P],
                                                       rope_d[j % 2][:, v, :, :].rearrange("p a d -> p (a d)"),
                                                       id_f[:, :])
                        last.then_inc(qk_turned, 1)

                    def scores(x):
                        j, u = x
                        head, t = row(j)
                        q = qk_hi[:, head, t * P:(t + 1) * P]
                        n = unit_no(x)
                        k0, w = 512 * u, width(x) * P
                        dst = s_bank[n % 4][:, 0:w]
                        diag = x == row_units(j)[-1]
                        if u == 0:
                            pe.wait_ge(qk_lo_done, it * (2 * ROWS) + (2 * j + 2))
                        if n >= 4 or seq is not FIRST:
                            pe.wait_ge(exped, it * NU + (n - 3))
                        nc.tensor.matmul(dst, q, qk_hi[:, 2 + head, k0:k0 + w], start=True, stop=False)
                        last = nc.tensor.matmul(dst, q, k_lo[:, head, k0:k0 + w], start=False, stop=not diag)
                        if diag:
                            last = nc.tensor.matmul(dst[:, w - P:w], id_b[:, :], mask_b[:, :],
                                                    start=False, stop=True)
                        last.then_inc(scored, 1)

                    def turn_probs(x):
                        j, u = x
                        ring_free("turn", j, u)
                        pe.wait_ge(exped, it * NU + (unit_no(x) + 1))
                        for k in range(width(x)):
                            last = nc.tensor.transpose(bank("turn", j, u)[:, k * P:(k + 1) * P],
                                                       probs[:, j % 2, (4 * u + k) * P:(4 * u + k + 1) * P],
                                                       id_f[:, :])
                        last.then_inc(turned, 1)

                    def pv_part(c, part):
                        head, t0 = row(2 * c)
                        n = t0 + 2
                        if part == 0:
                            pe.wait_ge(p_lo, it * NU + units_to(2 * c + 1))
                            pe.wait_ge(v_lo, it * ROWS + (2 * c + 6))
                            if 2 * c - 2 in seq.rows:
                                pe.wait_ge(o_out, it * COUPLES + c)
                        k0, k1 = (n * sum(PV_PARTS[:p]) // sum(PV_PARTS) for p in (part, part + 1))
                        for k in range(k0, k1):
                            c0 = P if k == n - 1 else 0
                            v = v_st[:, k, head, :, :].rearrange("p a d -> p (a d)")
                            for src in (pt_hi, pt_lo):
                                last = nc.tensor.matmul(o_ps[:, c0:2 * P], v, src[:, c % 2, k, c0:2 * P],
                                                        start=(k == 0 and src is pt_hi),
                                                        stop=(k == n - 1 and src is pt_lo),
                                                        skip_group_check=True)
                        if part == len(PV_PARTS) - 1:
                            last.then_inc(pv_done, 1)

                    def turn_out(c):
                        ring_free("out", 2 * c)
                        pe.wait_ge(o_out, it * COUPLES + (c + 1))
                        for a in range(2):
                            last = nc.tensor.matmul(bank("out", 2 * c)[:, a * DK:(a + 1) * DK],
                                                    o_sum[:, a * P:(a + 1) * P], id_2[:, :],
                                                    start=True, stop=True)
                        last.then_inc(o_turned, 1)

                    if seq is FIRST:
                        pe.wait_ge(a_lo, b * 8 + 8)
                    for i in seq.steps:
                        tr, sc = seq.units(i, TURN), seq.units(i, 0)
                        late = sc[-1:] if last_scored_late(sc) else []
                        for x in tr[1:2]:
                            turn_probs(x)
                        for j in seq.tile(i, MUL):
                            multiply(j)
                        for k in range(4):
                            for c in seq.couple(i, PV):
                                if 4 * (i % 2) + k < len(PV_PARTS):
                                    pv_part(c, 4 * (i % 2) + k)
                            for x in sc[k:k + 1]:
                                if x not in late:
                                    scores(x)
                            for x in tr[k + 2:k + 3]:
                                turn_probs(x)
                            if k == 0:
                                for j in seq.tile(i, TURN_QK):
                                    turn_qk(j)
                            if k == 1:
                                for c in seq.final(i):
                                    turn_out(c)
                            if k == 2:
                                for x in seq.units(i, EXP)[0:1]:
                                    turn_probs(x)
                        for x in late:
                            scores(x)
                        for k in early_chunks(seq, i):
                            if k == 0:
                                pe.wait_ge(exped, it * NU + NU)
                            turn_attn(b * GROUPS, k, gu_bank)

                run(FIRST, b * PAIRS)
                with pe.Fori(1, PAIRS - 1) as pr:
                    run(MIDDLE, b * PAIRS + pr)
                run(LAST, b * PAIRS + (PAIRS - 1))

                def project_out(c, t0, t1):
                    for t in range(t0, t1):
                        for k in range(OC):
                            last = product(y_ps[:, t * DM:(t + 1) * DM],
                                           [x[:, 512 * k + t * P:512 * k + (t + 1) * P] for x in o_t],
                                           [x[:, k * DM:(k + 1) * DM] for x in wo_hl],
                                           first=(k == 0), last=(k == OC - 1))
                    if t1 == TG:
                        last.then_inc(y_done, 1)

                def turn_x1(c):
                    pe.wait_ge(ln_rows, c * TG + TG)
                    for k in range(KC):
                        for t in range(TG):
                            last = nc.tensor.transpose(gu_bank[k][:, t * P:(t + 1) * P],
                                                       x1_g[:, t * DM + k * P:t * DM + (k + 1) * P], id_f[:, :])
                        last.then_inc(x_turned, 1)

                def ffn_up(c, turns):
                    pe.wait_ge(x_lo, c * KC + KC)
                    pe.wait_ge(cw_lo, b * 4 + 4)
                    for m in range(MC):
                        if m >= 2:
                            pe.wait_ge(hid_done, c * MC + (m - 1))
                        for dst, w in ((gu_bank[2 - 2 * (m % 2)], wg_hl), (gu_bank[3 - 2 * (m % 2)], wu_hl)):
                            for k in range(KC):
                                last = product(dst, [x[:, k * HID + m * P:k * HID + (m + 1) * P] for x in w],
                                               [x[:, 512 * k:512 * (k + 1)] for x in x1_t],
                                               first=(k == 0), last=(k == KC - 1))
                        last.then_inc(gate_up, 1)
                        if turns:
                            if m == 0:
                                pe.wait_ge(x_added, c + 2)
                            turn_attn(c + 2, m, y_bank)
                    if turns:
                        for k in range(MC, OC):
                            turn_attn(c + 2, k, y_bank)

                def ffn_down(c):
                    pe.wait_ge(hid_lo, c * MC + MC)
                    pe.wait_ge(z_added, c + 1)
                    for t in range(TG):
                        for m in range(MC):
                            last = product(z_ps[:, t * DM:(t + 1) * DM],
                                           [x[:, 512 * m + t * P:512 * m + (t + 1) * P] for x in hid_t],
                                           [x[:, m * DM:(m + 1) * DM] for x in wd_hl],
                                           first=(m == 0), last=(m == MC - 1))
                    last.then_inc(z_done, 1)

                def group(c, turns):
                    pe.wait_ge(c_lo, c * OC + 2 * OC)
                    project_out(c + 1, 0, TG // 2)
                    turn_x1(c)
                    project_out(c + 1, TG // 2, TG)
                    ffn_up(c, turns)
                    ffn_down(c)

                c = b * GROUPS
                pe.wait_ge(cw_lo, b * 4 + 1)
                pe.wait_ge(c_lo, c * OC + OC)
                project_out(c, 0, TG)
                for k in range(OC):
                    turn_attn(c + 1, k, gu_bank)
                with pe.Fori(0, GROUPS - 2) as g:
                    group(b * GROUPS + g, True)
                c = b * GROUPS + (GROUPS - 2)
                group(c, False)
                turn_x1(c + 1)
                ffn_up(c + 1, False)
                ffn_down(c + 1)


_INS = ["h", "gamma", "beta", "wqkv", "bqkv", "wo", "bo", "wgate_t", "wup_t", "wdown_t",
        "cos", "sin", "ident", "ident2", "mask"]


def kernel(L0_attn_h, L0_attn_gamma, L0_attn_beta, L0_attn_Wq, L0_attn_bq, L0_attn_Wk, L0_attn_bk,
           L0_attn_Wv, L0_attn_bv, L0_attn_Wo, L0_attn_bo, L0_ffn_w_gate, L0_ffn_w_up, L0_ffn_w_down):
    import ml_dtypes
    import numpy as np
    import concourse.bacc as bacc
    from concourse.bass_utils import run_bass_kernel_spmd

    theta = np.float32(1.0) / np.float32(10000.0) ** (np.arange(0, DK, 2, dtype=np.float32) / np.float32(DK))
    angle = np.arange(SEQ, dtype=np.float32)[:, None] * theta[None, :].astype(np.float32)
    tiled = angle.reshape(TT, P, DK // 2).transpose(1, 0, 2)
    eye = np.eye(P, dtype=np.float32)
    later = np.triu(np.full((P, P), MASKED, np.float32), 1)

    arrays = {
        "h": L0_attn_h, "gamma": np.reshape(L0_attn_gamma, (KC, P)).T, "beta": np.reshape(L0_attn_beta, (KC, P)).T,
        "wqkv": np.stack([L0_attn_Wq, L0_attn_Wk, L0_attn_Wv]),
        "bqkv": np.stack([L0_attn_bq, L0_attn_bk, L0_attn_bv]),
        "wo": L0_attn_Wo, "bo": L0_attn_bo,
        "wgate_t": np.transpose(L0_ffn_w_gate), "wup_t": np.transpose(L0_ffn_w_up),
        "wdown_t": np.transpose(L0_ffn_w_down),
        "cos": np.cos(tiled).astype(np.float32), "sin": np.sin(tiled).astype(np.float32),
        "ident": eye, "ident2": np.concatenate([eye[:DK, :DK]] * 2),
        "mask": np.stack([eye, later]).astype(ml_dtypes.bfloat16),
    }
    arrays = {n: np.ascontiguousarray(a) for n, a in arrays.items()}
    nc = bacc.Bacc("TRN2", target_bir_lowering=False, num_devices=1)
    args = [nc.dram_tensor(f"in_{n}", arrays[n].shape, mybir.dt.from_np(arrays[n].dtype),
                           kind="ExternalInput").ap() for n in _INS]
    attn = nc.dram_tensor("attn", (BATCH, SEQ, HEADS * DK), F32, kind="Internal").ap()
    out = nc.dram_tensor("out", (BATCH, SEQ, DM), F32, kind="ExternalOutput").ap()
    postln_block_kernel(nc, *args, attn, out)
    r = run_bass_kernel_spmd(nc, [{f"in_{n}": arrays[n] for n in _INS}], core_ids=[0])
    return r.results[0]["out"]
```
